# Optimizing a Trainium2 kernel written in Bass

```python
import numpy as np
import jax
import jax.numpy as jnp

def _softmax(x, axis=-1):
    return jax.nn.softmax(x, axis=axis)

def _gelu(x):
    return jax.nn.gelu(x, approximate=True)

def _silu(x):
    return jax.nn.silu(x)

def _sigmoid(x):
    return jax.nn.sigmoid(x)

def _layernorm(x, axis=-1, eps=1e-05):
    m = jnp.mean(x, axis=axis, keepdims=True)
    v = jnp.var(x, axis=axis, keepdims=True)
    return (x - m) / jnp.sqrt(v + eps)

def _scatter_add(tgt, idx, src, axis=0):
    return tgt.at[idx].add(src)

def _segment_sum(src, seg, n):
    return jax.ops.segment_sum(src, seg, n)
kernel_name = 'mk_gnn_ffn_d1_gnn_r8_29dce1'

def setup_inputs(seed: int=0):
    np.random.seed(seed)
    _w = jnp.asarray

    def _rec_inputs():
        import jax
        import jax.numpy as jnp
        _gk = jax.random.key(seed)
        x = -8.776e-05 + 1 * jax.random.normal(jax.random.fold_in(_gk, 1), (1250, 512), jnp.float32)
        src = jax.random.randint(jax.random.fold_in(_gk, 2), (20000,), 0, 1250, jnp.int32)
        dst = jnp.minimum((1250 * jax.random.uniform(jax.random.fold_in(_gk, 3), (20000,)) ** 2.0).astype(jnp.int32), 9999)
        _o = jnp.argsort(dst, stable=True)
        src = src[_o]
        dst = dst[_o]
        edge_attr_512 = -8.513e-05 + 0.999844 * jax.random.normal(jax.random.fold_in(_gk, 11), (20000, 512), jnp.float32)
        return (x, src, dst, edge_attr_512)
    x, src, dst, edge_attr_512 = _rec_inputs()

    def _L0_gnn_setup():
        import jax, jax.numpy as jnp
        import numpy as np
        N = 1250
        E = 20000
        D = 512
        key = jax.random.key(seed)
        k1, k2, k3, k4, k5 = jax.random.split(key, 5)
        node_tokens = jax.random.normal(k1, (N, D), dtype=jnp.float32)
        relation_tokens = jax.random.normal(k2, (E, D), dtype=jnp.float32)
        edge_index = jax.random.randint(k3, (2, E), 0, N, dtype=jnp.int64)
        lim_m = float(np.sqrt(6.0 / (D + D)))
        Wm = jax.random.uniform(k4, (D, D), minval=-lim_m, maxval=lim_m, dtype=jnp.float32)
        bm = jnp.zeros((D,), dtype=jnp.float32)
        lim_u = float(np.sqrt(6.0 / (2 * D + D)))
        Wu = jax.random.uniform(k5, (D, 2 * D), minval=-lim_u, maxval=lim_u, dtype=jnp.float32)
        bu = jnp.zeros((D,), dtype=jnp.float32)
        gamma = jnp.ones((D,), dtype=jnp.float32)
        beta = jnp.zeros((D,), dtype=jnp.float32)
        return {'node_tokens': node_tokens, 'relation_tokens': relation_tokens, 'edge_index': edge_index, 'num_nodes': N, 'Wm': Wm, 'bm': bm, 'Wu': Wu, 'bu': bu, 'gamma': gamma, 'beta': beta}
    _L0_gnn_all = _L0_gnn_setup()
    _L0_gnn_in = {k: v for k, v in _L0_gnn_all.items() if k in ('Wm', 'bm', 'Wu', 'bu', 'gamma', 'beta')}
    del _L0_gnn_all

    def _L0_ffn_setup():
        import jax, jax.numpy as jnp
        import numpy as np
        from jax import lax
        N, M, DIM, HEADS, TOPK = (4, 256, 512, 8, 16)

        def _split_heads(t, h):
            n, m, c = t.shape
            return t.reshape(n, m, h, c // h).transpose(0, 2, 1, 3).reshape(n * h, m, c // h)
        key = jax.random.key(seed)
        ks = jax.random.split(key, 7)
        f = lambda k, s, sc=1.0: jax.random.normal(k, s, dtype=jnp.float32) * sc
        return {'x': f(ks[0], (N, M, DIM)), 'pos_w': f(ks[1], (DIM, 1, 3), 0.1), 'pos_b': f(ks[2], (DIM,), 0.02), 'qkv_w': f(ks[3], (3 * DIM, DIM), 0.02), 'qkv_b': f(ks[4], (3 * DIM,), 0.02), 'wo_w': f(ks[5], (DIM, DIM), 0.02), 'wo_b': f(ks[6], (DIM,), 0.02)}
    _L0_ffn_all = _L0_ffn_setup()
    _L0_ffn_in = {k: v for k, v in _L0_ffn_all.items() if k in ('pos_w', 'pos_b', 'qkv_w', 'qkv_b', 'wo_w', 'wo_b')}
    del _L0_ffn_all
    return {'x': x, 'src': src, 'dst': dst, 'edge_attr_512': edge_attr_512, 'L0_gnn_Wm': _L0_gnn_in['Wm'], 'L0_gnn_bm': _L0_gnn_in['bm'], 'L0_gnn_Wu': _L0_gnn_in['Wu'], 'L0_gnn_bu': _L0_gnn_in['bu'], 'L0_gnn_gamma': _L0_gnn_in['gamma'], 'L0_gnn_beta': _L0_gnn_in['beta'], 'L0_ffn_pos_w': _L0_ffn_in['pos_w'], 'L0_ffn_pos_b': _L0_ffn_in['pos_b'], 'L0_ffn_qkv_w': _L0_ffn_in['qkv_w'], 'L0_ffn_qkv_b': _L0_ffn_in['qkv_b'], 'L0_ffn_wo_w': _L0_ffn_in['wo_w'], 'L0_ffn_wo_b': _L0_ffn_in['wo_b']}

def reference(x, src, dst, edge_attr_512, L0_gnn_Wm, L0_gnn_bm, L0_gnn_Wu, L0_gnn_bu, L0_gnn_gamma, L0_gnn_beta, L0_ffn_pos_w, L0_ffn_pos_b, L0_ffn_qkv_w, L0_ffn_qkv_b, L0_ffn_wo_w, L0_ffn_wo_b):
    import jax
    import jax.numpy as jnp

    def _L0_gnn_ref(node_tokens, relation_tokens, edge_index, num_nodes, Wm, bm, Wu, bu, gamma, beta):
        import jax, jax.numpy as jnp
        import numpy as np
        N = 1250
        E = 20000
        D = 512
        head = edge_index[0]
        tail = edge_index[1]
        msg = node_tokens[head] + relation_tokens
        msg = msg @ Wm.T + bm
        agg = jax.ops.segment_sum(msg, tail, num_segments=num_nodes)
        deg = jax.ops.segment_sum(jnp.ones((msg.shape[0],), dtype=msg.dtype), tail, num_segments=num_nodes)
        agg = agg / jnp.maximum(deg, 1.0)[:, None]
        update_in = jnp.concatenate((node_tokens, agg), axis=-1)
        update = update_in @ Wu.T + bu
        out = node_tokens + jax.nn.gelu(update, approximate=False)
        mean = jnp.mean(out, axis=-1, keepdims=True)
        var = jnp.var(out, axis=-1, keepdims=True)
        return (out - mean) / jnp.sqrt(var + 1e-05) * gamma + beta

    def _L0_ffn_ref(x, pos_w, pos_b, qkv_w, qkv_b, wo_w, wo_b):
        import jax, jax.numpy as jnp
        import numpy as np
        from jax import lax
        N, M, DIM, HEADS, TOPK = (4, 256, 512, 8, 16)

        def _split_heads(t, h):
            n, m, c = t.shape
            return t.reshape(n, m, h, c // h).transpose(0, 2, 1, 3).reshape(n * h, m, c // h)
        n, m, c = x.shape
        h = HEADS
        scale = c ** (-0.5)
        pos = lax.conv_general_dilated(x.transpose(0, 2, 1), pos_w, window_strides=(1,), padding=[(1, 1)], feature_group_count=c, dimension_numbers=('NCH', 'OIH', 'NCH'))
        x = x + (pos + pos_b[None, :, None]).transpose(0, 2, 1)
        qkv = x @ qkv_w.T + qkv_b
        q, k, v = jnp.split(qkv, [c, 2 * c], axis=-1)
        q = _split_heads(q, h)
        k = _split_heads(k, h)
        v = _split_heads(v, h)
        qd = lax.stop_gradient(q)
        kd = lax.stop_gradient(k)
        logits = jnp.einsum('bmd,bpd->bmp', qd * scale, kd)
        _, idx = lax.top_k(logits, TOPK)
        gather = jax.vmap(lambda t, i: t[i])
        k_sel = gather(k, idx)
        v_sel = gather(v, idx)
        attn = jax.nn.softmax(jnp.einsum('bmd,bmkd->bmk', q * scale, k_sel), axis=-1)
        out = jnp.einsum('bmk,bmkd->bmd', attn, v_sel)
        d = c // h
        out = out.reshape(n, h, m, d).transpose(0, 2, 1, 3).reshape(n, m, c)
        return out @ wo_w.T + wo_b
    edge_index = jnp.stack([src, dst])
    x = x + _L0_gnn_ref(_layernorm(x, axis=-1), edge_attr_512, edge_index, 1250, L0_gnn_Wm, L0_gnn_bm, L0_gnn_Wu, L0_gnn_bu, L0_gnn_gamma, L0_gnn_beta)
    x = x + _L0_ffn_ref(_layernorm(x, axis=-1)[None], L0_ffn_pos_w, L0_ffn_pos_b, L0_ffn_qkv_w, L0_ffn_qkv_b, L0_ffn_wo_w, L0_ffn_wo_b)[0]
    return x

_drawn_inputs = setup_inputs


def setup_inputs(seed=0):
    import zlib

    import numpy as np

    out = dict(_drawn_inputs(seed))
    spreads = {'L0_gnn_bm': (0.0, 0.314),
     'L0_gnn_bu': (0.0, 0.1),
     'L0_gnn_gamma': (1.0, 0.2),
     'L0_gnn_beta': (0.0, 0.1)}
    factors = {'L0_ffn_pos_w': 3.382, 'L0_ffn_pos_b': 8.0, 'L0_ffn_qkv_b': 6.978, 'L0_ffn_wo_b': 5.382}
    for name, (base, spread) in spreads.items():
        noise = np.random.default_rng([zlib.crc32(name.encode()), seed]).standard_normal(out[name].shape)
        drawn = base * np.exp(spread * noise) if base else spread * noise
        out[name] = jnp.asarray(drawn.astype(out[name].dtype))
    for name, factor in factors.items():
        out[name] = (out[name] * factor).astype(out[name].dtype)
    return out
```

```python
from contextlib import ExitStack

import concourse.bass as bass
from concourse import mybir

F32 = mybir.dt.float32
F16 = mybir.dt.float16
I32 = mybir.dt.int32
U32 = mybir.dt.uint32
ALU = mybir.AluOpType
ACT = mybir.ActivationFunctionType
AX = mybir.AxisListType

P = 128
BANK = 512
EPS = 1e-5
REMOVED = -3.0e38


def gnn_ffn(nc, x, src, dst, edge, Wm, bm, Wu, bu, gamma, beta, pos_w, pos_b, qkv_w, qkv_b, wo_w, wo_b, out):
    N, D = x.shape
    E = edge.shape[0]
    TP = 125
    NT = N // TP
    FC = D // P
    HEADS, HD = 8, 64
    G = 2
    BE = G * P
    NB = -(-E // BE)
    LAST = E - BE
    SEEN = (NB - 1) * BE - LAST
    R = 4
    PATH = 88
    ALL = 792
    TAB = 800
    SCALE = float(D) ** -0.5
    VW = HD + 1
    assert NT * TP == N and D == FC * P and SEEN % G == 0
    assert PATH >= NB + NT - 1 and PATH % R == 0 and ALL >= NB * NT and (ALL - PATH) % R == 0

    x_v = x.rearrange("(t p) d -> p t d", p=TP)
    out_v = out.rearrange("(t p) d -> t p d", p=TP)
    xn_d = nc.dram_tensor("xn_rows", (N, D), F32).ap()
    xn_v = xn_d.rearrange("(t p) d -> p t d", p=TP)
    row = lambda v: v.rearrange("(a d) -> a d", a=1)
    col = lambda v: v.rearrange("(c p) -> p c", p=P)

    def tile_of(ap, t):
        if isinstance(t, int):
            return ap[:, t, :]
        return ap[:, bass.ds(t, 1), :].rearrange("p a d -> p (a d)")

    def wait(eng, sem, value):
        if not (isinstance(value, int) and value <= 0):
            eng.wait_ge(sem, value)

    with ExitStack() as whole:
        def sem(name):
            return whole.enter_context(nc.semaphore(name))

        def sb(name, shape, dt=F32, stack=whole):
            return stack.enter_context(nc.sbuf_tensor(name, shape, dt))

        ps = whole.enter_context(nc.psum_tensor("ps", [P, 8 * BANK], F32))

        def bank(b, n=BANK, parts=P):
            return ps[0:parts, b * BANK:b * BANK + n]

        x_sb = sb("x_sb", [TP, NT, D])
        wqkvT = sb("wqkvT", [P, FC, 3 * D])
        woT = sb("woT", [P, FC, D])
        xaT = sb("xaT", [P, FC, N])
        wu2T = xaT[:, :, :].rearrange("p c n -> p (c n)")[:, 0:FC * D].rearrange("p (c n) -> p c n", c=FC)
        gamma_b = sb("gamma_b", [TP, D])
        beta_b = sb("beta_b", [TP, D])
        wob_b = sb("wob_b", [TP, D])
        vb_b = sb("vb_b", [TP, D])
        ident = sb("ident", [P, P])
        ones = sb("ones", [P, P])
        qkb = sb("qkb", [P, 2 * FC])
        qb = sb("qb", [P, FC])
        cw = sb("cw", [P, FC, 3])
        cw1 = sb("cw1", [P, FC])
        pb = sb("pb", [P, FC])
        bmc = sb("bmc", [P, FC])
        brhs = sb("brhs", [33, D])

        gnn = ExitStack()
        g_sb = lambda n, s, d=F32: sb(n, s, d, gnn)
        xn = g_sb("xn", [TP, NT, D])
        acc = g_sb("acc", [TP, NT, D + 1])
        w1T = g_sb("w1T", [P, FC, D])
        w2T = g_sb("w2T", [P, FC, D])
        natA = g_sb("natA", [P, 8, D])
        natB = g_sb("natB", [P, 4, D])
        ring = g_sb("ring", [P, R, G * D])
        onehot = g_sb("onehot", [P, R, G, TP])
        iota_n = g_sb("iota_n", [P, NT, TP], F16)
        tab_b = g_sb("tab_b", [1, TAB], I32)
        tab_e = g_sb("tab_e", [1, TAB], I32)
        tab_t = g_sb("tab_t", [1, TAB], I32)
        dst_i = g_sb("dst_i", [P, NB + 1, G], I32)
        dst_f = g_sb("dst_f", [P, NB + 1, G])
        src_i = g_sb("src_i", [P, NB + 1, G], I32)
        idx = g_sb("idx", [P, R, G], I32)
        seq_a = g_sb("seq_a", [TP, E // TP], I32)
        seq_b = g_sb("seq_b", [TP, E // TP], I32)
        falls = g_sb("falls", [TP, E // TP])
        fall = g_sb("fall", [TP, 1])
        dl_i = g_sb("dl_i", [1, NB], I32)
        dl_f = g_sb("dl_f", [1, NB])
        thr = g_sb("thr", [PATH, NB])
        below = g_sb("below", [PATH, NB])
        stepped = g_sb("stepped", [PATH, 1])
        rows = g_sb("rows", [1, 6, PATH])
        flag_f = g_sb("flag_f", [1, 1])
        flag_i = g_sb("flag_i", [1, 1], I32)
        mv = g_sb("mv", [TP, NT, 2])
        st6 = g_sb("st6", [TP, NT, 6])
        sd = g_sb("sd", [TP, NT])
        rs = g_sb("rs", [TP, NT])
        xs = natA[0:TP, 4:6, :]
        sc = natA[0:TP, 6:8, :]
        lT = natB[:, :, :].rearrange("p a n -> p (a n)")[:, 0:4 * FC * TP]\
            .rearrange("p (u c n) -> p u c n", u=2, c=2 * FC)
        blhs = g_sb("blhs", [33, 2, TP])
        tiny = g_sb("tiny", [TP, 2, 16])
        gnn.close()

        ffn = ExitStack()
        f_sb = lambda n, s, d=F32: sb(n, s, d, ffn)
        xcT = f_sb("xcT", [P, FC, N + TP])
        kT = f_sb("kT", [P, FC, N])
        v_sb = f_sb("v_sb", [TP, NT, HEADS * VW])
        qcur = f_sb("qcur", [P, 2, FC, TP])
        eS = f_sb("eS", [TP, 2, N])
        rS = f_sb("rS", [TP, 2, N])
        pT = f_sb("pT", [TP, 2, NT, TP])
        o_sb = f_sb("o_sb", [TP, 2, D])
        oT = f_sb("oT", [P, 2, FC, TP])
        res = f_sb("res", [TP, 2, D])
        top = f_sb("top", [TP, 2, 16])
        rinv = f_sb("rinv", [TP, 2, 1])
        negm = f_sb("negm", [TP, 2, 1])
        sS = xaT[0:TP, :, :].rearrange("p c n -> p (c n)")[:, 0:2 * N].rearrange("p (s n) -> p s n", s=2)
        ffn.close()

        x_in = [sem(f"x_in{i}") for i in range(2)]
        idx_in = sem("idx_in")
        small_in = sem("small_in")
        wu_in = sem("wu_in")
        wm_in = sem("wm_in")
        wq_in = sem("wq_in")
        wq2_in = sem("wq2_in")
        wo_in = sem("wo_in")
        xn_out = sem("xn_out")
        consts = sem("consts")
        padded = sem("padded")
        seqpad = sem("seqpad")
        ixd = sem("ixd")
        ixp = sem("ixp")
        tabs = sem("tabs")
        st_d = sem("st_d")
        sd_done = sem("sd_done")
        xn_done = sem("xn_done")
        xb_done = sem("xb_done")
        wt_ps = sem("wt_ps")
        wt_sb = sem("wt_sb")
        sums = sem("sums")
        load_done = [sem(f"load_done{i}") for i in range(R)]
        gather_done = [sem(f"gather_done{i}") for i in range(R)]
        idx_done = sem("idx_done")
        hot_done = sem("hot_done")
        adds = sem("adds")
        agg_done = sem("agg_done")
        p_gate, v_gate, a_gate, t_gate = sem("p_gate"), sem("v_gate"), sem("a_gate"), sem("t_gate")
        xs_done = sem("xs_done")
        sc_done = sem("sc_done")
        ud = sem("ud")
        upT = sem("upT")
        ulT = sem("ulT")
        u_ps = sem("u_ps")
        gelu_done = sem("gelu_done")
        ve_done = sem("ve_done")
        sq_done = sem("sq_done")
        x1_done = sem("x1_done")
        x1b_done = sem("x1b_done")
        xa_done = sem("xa_done")
        xaT_ps = sem("xaT_ps")
        xaT_sb = sem("xaT_sb")
        cv = sem("cv")
        xc_done = sem("xc_done")
        vones = sem("vones")
        k_ps = sem("k_ps")
        k_sb = sem("k_sb")
        v_ps = sem("v_ps")
        v_done = sem("v_done")
        q_ps = sem("q_ps")
        q_sb = sem("q_sb")
        s_ps = sem("s_ps")
        s_sb = sem("s_sb")
        max1 = sem("max1")
        rep1 = sem("rep1")
        max2 = sem("max2")
        rep2 = sem("rep2")
        m_done = sem("m_done")
        e_done = sem("e_done")
        r_done = sem("r_done")
        p_done = sem("p_done")
        pT_ps = sem("pT_ps")
        pT_sb = sem("pT_sb")
        o_ps = sem("o_ps")
        inv_done = sem("inv_done")
        o_done = sem("o_done")
        oT_ps = sem("oT_ps")
        oT_sb = sem("oT_sb")
        y_ps = sem("y_ps")
        y_done = sem("y_done")
        y_out = [sem("y_out0"), sem("y_out1")]

        def gate(eng, s):
            eng.sem_inc(s, 1)

        EPN = E // TP
        block = whole.enter_context(nc.Block())

        @block.sync
        def _(sp):
            for h in range(2):
                t0, t1 = h * NT // 2, (h + 1) * NT // 2
                for a, b in ((0, 120), (120, TP)):
                    sp.dma_start(x_sb[a:b, t0:t1, :], x_v[a:b, t0:t1, :]).then_inc(x_in[h], 16)
            sp.dma_start(natA[:, 0:8, :].rearrange("p a n -> p (a n)").rearrange("p (c f) -> p c f", c=FC),
                         Wu.rearrange("(c p) f -> p c f", p=P)).then_inc(wu_in, 16)
            sp.dma_start(natB[:, :, :], Wm.rearrange("(c p) f -> p c f", p=P)).then_inc(wm_in, 16)
            sp.wait_ge(xn_done, NT)
            for a, b in ((0, 120), (120, TP)):
                sp.dma_start(xn_v[a:b, :, :], xn[a:b, :, :]).then_inc(xn_out, 16)
            sp.wait_ge(tabs, 1)

            def load_items(first, end):
                with sp.Fori(first, end, R) as i:
                    for r in range(R):
                        e0 = sp.value_load(tab_e[0:1, bass.ds(i + r, 1)], min_val=0, max_val=LAST)
                        sp.wait_ge(sums, i + (r + 1))
                        sp.dma_start(ring[:, r, :], edge[bass.ds(e0, BE), :].rearrange("(p g) d -> p (g d)", g=G))\
                            .then_inc(load_done[r], 16)

            load_items(0, PATH)
            unsorted = sp.value_load(flag_i[0:1, 0:1], min_val=0, max_val=1)
            with sp.If(unsorted > 0):
                load_items(PATH, ALL)
            sp.end_ifs()

            def store(t, u):
                sp.wait_ge(y_done, t + 1)
                dst_rows = out_v[t] if isinstance(t, int) else out_v[bass.ds(t, 1)].rearrange("a p d -> (a p) d")
                sp.dma_start(dst_rows, res[:, u, :]).then_inc(y_out[u], 16)

            with sp.Fori(0, NT // 2) as pair:
                for u in range(2):
                    store(2 * pair + u, u)
            for u in range(2):
                sp.wait_ge(y_out[u], 16 * NT // 2)

        @block.gpsimd
        def _(pl):
            pl.memset(ident[:, :], 0.0).then_inc(consts, 1)
            pl.memset(ones[:, :], 1.0).then_inc(consts, 1)
            pl.memset(seq_b[:, :], 1 << 20).then_inc(seqpad, 1)
            pl.wait_ge(consts, 1)
            pl.affine_select(out=ident[:, :], in_=ident[:, :], compare_op=ALU.not_equal, fill=1.0, base=0,
                             pattern=[[-1, P]], channel_multiplier=1).then_inc(consts, 1)
            pl.iota(thr[:, :], pattern=[[-TP, NB]], base=0, channel_multiplier=TP,
                    allow_small_or_imprecise_dtypes=True).then_inc(consts, 1)
            pl.iota(tab_b[0:1, :], pattern=[[1, TAB // NT], [0, NT]], base=0, channel_multiplier=0).then_inc(consts, 1)
            pl.iota(tab_t[0:1, :], pattern=[[0, TAB // NT], [1, NT]], base=0, channel_multiplier=0).then_inc(consts, 1)
            pl.iota(rows[0:1, 0, :], pattern=[[1, PATH]], base=0, channel_multiplier=0,
                    allow_small_or_imprecise_dtypes=True).then_inc(consts, 1)
            pl.iota(iota_n[:, :, :], pattern=[[TP, NT], [1, TP]], base=0, channel_multiplier=0,
                    allow_small_or_imprecise_dtypes=True).then_inc(consts, 1)
            pl.memset(blhs[:, :, :], 0.0).then_inc(consts, 1)
            pl.memset(brhs[:, :], 0.0).then_inc(consts, 1)
            pl.wait_ge(consts, 10)
            pl.memset(blhs[0:1, :, :], 1.0).then_inc(consts, 1)
            pl.wait_ge(idx_in, 16 * 9)
            pl.wait_ge(ixd, 2)
            pl.affine_select(out=dst_f[:, NB - 1, :], in_=dst_f[:, NB - 1, :], compare_op=ALU.is_ge, fill=-1.0,
                             base=-(SEEN // G), pattern=[[0, G]], channel_multiplier=1).then_inc(padded, 1)
            pl.memset(dst_f[:, NB, :], -1.0).then_inc(padded, 1)
            pl.tensor_copy(src_i[:, NB, :], src_i[:, NB - 1, :]).then_inc(padded, 1)
            pl.wait_ge(padded, 3)
            pl.wait_ge(tabs, 1)
            pl.wait_ge(xn_out, 32)

            def gather_items(first, end):
                with pl.Fori(first, end, R) as i:
                    for r in range(R):
                        b = pl.value_load(tab_b[0:1, bass.ds(i + r, 1)], min_val=0, max_val=NB)
                        pl.wait_ge(load_done[r], 16 * (i // R) + 16)
                        pl.tensor_copy(idx[:, r, :], tile_of(src_i, b)).then_inc(idx_done, 1)
                        pl.wait_ge(idx_done, i + (r + 1))
                        gate(pl, p_gate)
                        for g in range(G):
                            pl.indirect_dma_start(ring[:, r, g * D:(g + 1) * D], None, xn_d[:, :],
                                                  bass.IndirectOffsetOnAxis(ap=idx[:, r, g:g + 1].bitcast(U32), axis=0),
                                                  compute_op=ALU.add).then_inc(gather_done[r], 16)

            gather_items(0, PATH)
            unsorted = pl.value_load(flag_i[0:1, 0:1], min_val=0, max_val=1)
            with pl.If(unsorted > 0):
                gather_items(PATH, ALL)
            pl.end_ifs()
            pl.wait_ge(wt_sb, 4)
            for t in range(NT):
                pl.tensor_tensor(x_sb[:, t, :], x_sb[:, t, :], beta_b[:, :], ALU.add).then_inc(xb_done, 1)

            def keep_x1(t, u):
                pl.wait_ge(x1_done, t + 1)
                gate(pl, p_gate)
                pl.tensor_tensor(tile_of(x_sb, t), xs[:, u, :], wob_b[:, :], ALU.add).then_inc(x1b_done, 1)

            with pl.Fori(0, NT // 2) as pair:
                for u in range(2):
                    keep_x1(2 * pair + u, u)
            pl.wait_ge(xaT_sb, NT)
            pl.wait_ge(x1b_done, NT)
            pl.memset(v_sb[:, :, :], 1.0).then_inc(vones, 1)
            pl.memset(xcT[:, :, N:N + TP], 0.0).then_inc(vones, 1)

            def weights(n, s):
                pl.wait_ge(e_done, n + 1)
                pl.wait_ge(r_done, n + 1)
                gate(pl, p_gate)
                pl.tensor_tensor(eS[:, s, :], eS[:, s, :], rS[:, s, :], ALU.subtract).then_inc(p_done, 1)

            with pl.Fori(0, NT * HEADS, 2) as n:
                for s in range(2):
                    weights(n + s, s)

        @block.scalar
        def _(act):
            row_in = lambda o, i: act.dma_start(o, i).then_inc(small_in, 16)
            act.wait_ge(seqpad, 1)
            ix = lambda o, i: act.dma_start(o, i, allow_slow_non_contiguous=True).then_inc(idx_in, 16)
            ix(seq_a[:, :], dst.rearrange("(p n) -> p n", p=TP))
            ix(seq_b[0:TP - 1, :], dst[1:1 + (TP - 1) * EPN].rearrange("(p n) -> p n", n=EPN))
            ix(seq_b[TP - 1:TP, 0:EPN - 1], row(dst[1 + (TP - 1) * EPN:E]))
            ix(dl_i[0:1, 0:NB - 1], dst[0:(NB - 1) * BE].rearrange("(a b) -> b a", b=BE)[BE - 1:BE, :])
            ix(dl_i[0:1, NB - 1:NB], row(dst[E - 1:E]))
            for tab, v in ((dst_i, dst), (src_i, src)):
                ix(tab[:, 0:NB - 1, :], v[0:(NB - 1) * BE].rearrange("(b p g) -> p b g", p=P, g=G))
                ix(tab[:, NB - 1, :], v[LAST:E].rearrange("(p g) -> p g", g=G))
            slow = lambda o, i: act.dma_start(o, i, allow_slow_non_contiguous=True).then_inc(small_in, 16)
            for j, v in enumerate((gamma, beta, wo_b, qkv_b[2 * D:3 * D])):
                row_in(w2T[0:1, j, :], row(v))
            act.wait_ge(consts, 11)
            row_in(brhs[0:1, :], row(bu))
            slow(qkb[:, :], col(qkv_b[0:2 * D]))
            slow(bmc[:, :], col(bm))
            slow(pb[:, :], col(pos_b))
            slow(cw[:, :, :], pos_w.rearrange("(c p) a k -> p c (a k)", p=P))
            act.wait_ge(small_in, 16 * 9)
            act.mul(qb[:, :], qkb[:, 0:FC], SCALE).then_inc(a_gate, 1)
            act.wait_ge(st_d, 2 * NT + 1)
            act.activation(sd[:, :], sd[:, :], ACT.Sqrt).then_inc(sd_done, 1)

            n = 0

            def evac(dst_ap, src_ap):
                nonlocal n
                n += 1
                act.wait_ge(wt_ps, n)
                act.activation(dst_ap, src_ap, ACT.Copy).then_inc(wt_sb, 1)

            B4 = lambda n: 4 + n % 4
            for k, o in enumerate((gamma_b, beta_b, wob_b, vb_b)):
                evac(o[:, :], bank(B4(k), D, TP))
            for c in range(FC):
                evac(w1T[:, c, :], bank(B4(4 + c)))
            for c in range(FC):
                evac(wu2T[:, c, :], bank(B4(8 + c)))
            act.dma_start(natA[:, :, :], qkv_w[0:8 * P, :].rearrange("(c p) f -> p c f", p=P)).then_inc(wq_in, 16)
            for c in range(FC):
                evac(w2T[:, c, :], bank(B4(12 + c)))
            act.dma_start(natB[:, :, :], qkv_w[8 * P:12 * P, :].rearrange("(c p) f -> p c f", p=P)).then_inc(wq2_in, 16)
            evac(brhs[32:33, :], ps[32:33, 4 * BANK:5 * BANK])
            k = 17
            for j in range(3):
                for c in range(FC):
                    evac(wqkvT[:, c, j * D:(j + 1) * D], bank(B4(k)))
                    k += 1
                if j == 1:
                    act.dma_start(natA[:, 0:4, :], wo_w.rearrange("(c p) f -> p c f", p=P)).then_inc(wo_in, 16)
            for c in range(FC):
                evac(woT[:, c, :], bank(B4(k)))
                k += 1

            def front(t, u):
                wait(act, x1b_done, t - 1)
                wait(act, xa_done, t - 1)
                if not isinstance(t, int):
                    gate(act, a_gate)
                act.activation(xs[:, u, :], tile_of(xn, t), ACT.Copy).then_inc(xs_done, 1)
                act.wait_ge(upT, 2 * t + 1)
                wait(act, u_ps, t - 1)
                act.activation(lT[:, u, 0:FC, :].rearrange("p a b -> p (a b)"), bank(4 * u, FC * TP), ACT.Copy)\
                    .then_inc(ulT, 1)
                act.wait_ge(upT, 2 * t + 2)
                act.activation(lT[:, u, FC:2 * FC, :].rearrange("p a b -> p (a b)"), bank(4 * u + 1, FC * TP),
                               ACT.Copy).then_inc(ulT, 1)
                act.activation(blhs[32:33, u, :], ps[32:33, (4 * u + 3) * BANK:(4 * u + 3) * BANK + TP],
                               ACT.Copy).then_inc(ulT, 1)

            def back(t, u):
                act.wait_ge(u_ps, t + 1)
                act.activation(sc[:, u, :], bank(4 * u + 2, D, TP), ACT.Gelu).then_inc(gelu_done, 1)
                for k in range(2):
                    act.wait_ge(ve_done, 2 * t + k + 1)
                    act.activation(tiny[:, u, 2 + 6 * k:3 + 6 * k], tiny[:, u, 2 + 6 * k:3 + 6 * k], ACT.Sqrt)\
                        .then_inc(sq_done, 1)
                act.wait_ge(xaT_ps, t + 1)
                if not isinstance(t, int):
                    gate(act, a_gate)
                    dst_cols = xaT[:, :, bass.ds(t * TP, TP)]
                else:
                    dst_cols = xaT[:, :, t * TP:(t + 1) * TP]
                act.activation(dst_cols, bank(4 * u + 3, FC * TP).rearrange("p (c n) -> p c n", c=FC), ACT.Copy)\
                    .then_inc(xaT_sb, 1)

            front(0, 0)
            front(1, 1)
            back(0, 0)
            with act.Fori(1, NT // 2) as pair:
                for u in range(2):
                    front(2 * pair + u, u)
                    back(2 * pair + (u - 1), 1 - u)
            back(NT - 1, (NT - 1) % 2)

            for c in range(FC):
                act.wait_ge(k_ps, c + 1)
                act.activation(kT[:, c, :], ps[:, 3 * (c % 2) * BANK:3 * (c % 2) * BANK + N], ACT.Identity,
                               bias=qkb[:, FC + c:FC + c + 1]).then_inc(k_sb, 1)

            def q_out(t, u):
                act.wait_ge(q_ps, t + 1)
                for c in range(FC):
                    ins = act.activation(qcur[:, u, c, :], ps[:, 7 * BANK + c * TP:7 * BANK + (c + 1) * TP],
                                         ACT.Identity, bias=qb[:, c:c + 1], scale=SCALE)
                ins.then_inc(q_sb, 1)

            def copy_logits(n, s):
                act.wait_ge(s_ps, n + 1)
                wait(act, e_done, n - 1)
                act.activation(sS[:, s, :], ps[0:TP, 0:N], ACT.Copy).then_inc(s_sb, 1)

            def exp_logits(n, s):
                act.wait_ge(rep1, n + 1)
                wait(act, r_done, n - 1)
                act.mul(negm[:, s, :], top[:, s, 0:1], -1.0).then_inc(m_done, 1)
                act.wait_ge(m_done, n + 1)
                act.wait_ge(s_sb, n + 1)
                wait(act, pT_ps, 3 * (n - 1))
                act.activation(eS[:, s, :], sS[:, s, :], ACT.Exp, bias=negm[:, s, :]).then_inc(e_done, 1)

            def exp_rest(n, s):
                act.wait_ge(rep2, n + 1)
                act.activation(rS[:, s, :], rS[:, s, :], ACT.Exp, bias=negm[:, s, :]).then_inc(r_done, 1)

            def weightsT(n, s):
                for g, (a, b) in enumerate(((0, 4), (4, 8), (8, NT))):
                    act.wait_ge(pT_ps, 3 * n + g + 1)
                    wait(act, o_ps, n - 1)
                    act.activation(pT[:, s, a:b, :].rearrange("p a b -> p (a b)"),
                                   bank(3 + g, (b - a) * TP, TP), ACT.Copy).then_inc(pT_sb, 1)

            def outT(t, u):
                act.wait_ge(oT_ps, t + 1)
                wait(act, y_ps, t - 1)
                act.activation(oT[:, u, :, :].rearrange("p a b -> p (a b)"), bank(7, FC * TP), ACT.Copy)\
                    .then_inc(oT_sb, 1)

            def tile(t, u, first=False):
                for h in range(HEADS):
                    n = HEADS * t + h
                    if h == HEADS - 1:
                        q_out(t + 1, 1 - u)
                    copy_logits(n + 1, 1 - h % 2)
                    exp_logits(n, h % 2)
                    if not (first and h == 0):
                        weightsT(n - 1, 1 - h % 2)
                    exp_rest(n, h % 2)
                    if h == 2 and not first:
                        outT(t - 1, 1 - u)

            q_out(0, 0)
            copy_logits(0, 0)
            tile(0, 0, True)
            tile(1, 1)
            with act.Fori(1, NT // 2) as pair:
                for u in range(2):
                    tile(2 * pair + u, u)
            weightsT(HEADS * NT - 1, 1)
            outT(NT - 1, (NT - 1) % 2)

        @block.vector
        def _(dv):
            dv.sem_inc(adds, 2)
            dv.wait_ge(idx_in, 16 * 9)
            dv.tensor_copy(dl_f[:, :], dl_i[:, :]).then_inc(ixd, 1)
            dv.tensor_copy(dst_f[:, 0:NB, :], dst_i[:, 0:NB, :]).then_inc(ixd, 1)
            dv.tensor_tensor(falls[:, :], seq_a[:, :], seq_b[:, :], ALU.is_gt).then_inc(ixd, 1)
            dv.wait_ge(ixd, 3)
            dv.tensor_reduce(fall[:, :], falls[:, :], AX.X, ALU.max).then_inc(ixd, 1)
            dv.wait_ge(ixp, 1)
            dv.wait_ge(consts, 7)
            dv.tensor_tensor(below[:, :], ps[0:PATH, 7 * BANK:7 * BANK + NB], thr[:, :], ALU.is_lt).then_inc(ixd, 1)
            dv.wait_ge(ixd, 5)
            dv.tensor_reduce(stepped[:, :], below[:, :], AX.X, ALU.add).then_inc(ixd, 1)
            dv.wait_ge(ixp, 2)
            dv.tensor_scalar(flag_f[:, :], ps[0:1, 6 * BANK:6 * BANK + 1], 1.0, None, ALU.min).then_inc(ixd, 1)
            dv.wait_ge(ixd, 7)
            dv.tensor_copy(flag_i[:, :], flag_f[:, :]).then_inc(ixd, 1)
            dv.wait_ge(ixp, 3)
            b_row, t_row, db, dt_, gb, gt = (rows[0:1, j, :] for j in (1, 2, 3, 4, 5, 5))
            dv.tensor_copy(b_row, ps[0:1, 5 * BANK:5 * BANK + PATH]).then_inc(ixd, 1)
            dv.wait_ge(ixd, 9)
            dv.tensor_tensor(t_row, rows[0:1, 0, :], b_row, ALU.subtract).then_inc(ixd, 1)
            dv.wait_ge(ixd, 10)
            dv.tensor_tensor(db, tab_b[0:1, 0:PATH], b_row, ALU.subtract).then_inc(ixd, 1)
            dv.tensor_tensor(dt_, tab_t[0:1, 0:PATH], t_row, ALU.subtract).then_inc(ixd, 1)
            dv.wait_ge(ixd, 12)
            dv.scalar_tensor_tensor(gb, db, flag_f[:, 0:1], b_row, ALU.mult, ALU.add).then_inc(ixd, 1)
            dv.wait_ge(ixd, 13)
            dv.tensor_copy(tab_b[0:1, 0:PATH], gb).then_inc(ixd, 1)
            dv.wait_ge(ixd, 14)
            dv.scalar_tensor_tensor(gt, dt_, flag_f[:, 0:1], t_row, ALU.mult, ALU.add).then_inc(ixd, 1)
            dv.wait_ge(ixd, 15)
            dv.tensor_scalar(tab_t[0:1, 0:PATH], gt, float(NT - 1), 0.0, ALU.min, ALU.max).then_inc(ixd, 1)
            dv.tensor_scalar(tab_e[0:1, :], tab_b[0:1, :], float(BE), float(LAST), ALU.mult, ALU.min).then_inc(ixd, 1)
            dv.wait_ge(ixd, 17)
            dv.memset(acc[:, :, :], 0.0).then_inc(tabs, 1)

            for t in range(NT):
                dv.wait_ge(x_in[t // (NT // 2)], 32)
                dv.bn_stats(st6[:, t, :], x_sb[:, t, :]).then_inc(st_d, 1)
            for t in range(NT):
                dv.wait_ge(st_d, t + 1)
                dv.bn_aggr(mv[:, t, :], st6[:, t, :]).then_inc(st_d, 1)
            dv.wait_ge(st_d, 2 * NT)
            dv.tensor_scalar(sd[:, :], mv[:, :, 1:2].rearrange("p a b -> p (a b)"), EPS, None, ALU.add)\
                .then_inc(st_d, 1)
            dv.wait_ge(sd_done, 1)
            dv.reciprocal(rs[:, :], sd[:, :]).then_inc(st_d, 1)
            dv.wait_ge(st_d, 2 * NT + 2)
            for t in range(NT):
                dv.tensor_scalar(xn[:, t, :], x_sb[:, t, :], mv[:, t, 0:1], rs[:, t:t + 1], ALU.subtract, ALU.mult)\
                    .then_inc(xn_done, 1)

            def hot(k, r, count):
                b = dv.value_load(tab_b[0:1, bass.ds(k, 1)], min_val=0, max_val=NB)
                j = dv.value_load(tab_t[0:1, bass.ds(k, 1)], min_val=0, max_val=NT - 1)
                wait(dv, sums, count)
                if not isinstance(count, int):
                    gate(dv, v_gate)
                for g in range(G):
                    ins = dv.tensor_scalar(onehot[:, r, g, :], tile_of(iota_n, j),
                                           dst_f[:, bass.ds(b, 1), g:g + 1].rearrange("p a b -> p (a b)"), None,
                                           ALU.is_equal)
                ins.then_inc(hot_done, 1)

            def add(k, r):
                j = dv.value_load(tab_t[0:1, bass.ds(k, 1)], min_val=0, max_val=NT - 1)
                dv.wait_ge(sums, k + (R + 1))
                dv.wait_ge(adds, k + 2)
                gate(dv, v_gate)
                dv.tensor_tensor(tile_of(acc, j), tile_of(acc, j), ps[0:TP, 2 * (r % 2) * BANK:2 * (r % 2) * BANK + D + 1],
                                 ALU.add).then_inc(adds, 1)

            def sum_items(first, end):
                with dv.Fori(first, end, R) as i:
                    for r in range(R):
                        hot(i + (r + 2), (r + 2) % R, i + (r + 3))
                        add(i + r, r)

            dv.wait_ge(padded, 3)
            dv.wait_ge(consts, 8)
            dv.wait_ge(tabs, 1)
            hot(0, 0, 0)
            hot(1, 1, 0)
            sum_items(0, PATH)
            dv.wait_ge(adds, PATH + 2)
            unsorted = dv.value_load(flag_i[0:1, 0:1], min_val=0, max_val=1)
            with dv.If(unsorted > 0):
                sum_items(PATH, ALL)
                dv.wait_ge(adds, ALL + 2)
            dv.end_ifs()
            dv.memset(tiny[:, :, :], 0.0).then_inc(agg_done, 1)
            dv.wait_ge(agg_done, 1)

            STEP = 11

            def front(t, u):
                cnt = tile_of(acc, t)[:, D:D + 1]
                base = 0 if isinstance(t, int) and t == 0 else STEP * t - (STEP - 3)
                wait(dv, xaT_ps, t - 1)
                if not isinstance(t, int):
                    gate(dv, v_gate)
                dv.tensor_scalar(tiny[:, u, 12:13], cnt, 1.0, None, ALU.max).then_inc(ud, 1)
                dv.tensor_scalar(tiny[:, u, 13:14], cnt, 1.0, None, ALU.min).then_inc(ud, 1)
                dv.wait_ge(ud, base + 2)
                dv.reciprocal(tiny[:, u, 14:15], tiny[:, u, 12:13]).then_inc(ud, 1)
                dv.wait_ge(ud, base + 3)
                gate(dv, v_gate)
                dv.tensor_scalar(sc[:, u, :], tile_of(acc, t)[:, 0:D], tiny[:, u, 14:15], None, ALU.mult)\
                    .then_inc(sc_done, 1)

            def back(t, u, ahead):
                base = STEP * t + 3 + ahead * 3

                def norm_stats(src_ap, k, b):
                    dv.bn_stats(st6[:, u, :], src_ap).then_inc(ud, 1)
                    dv.wait_ge(ud, b + 1)
                    gate(dv, v_gate)
                    dv.bn_aggr(tiny[:, u, 6 * k + 0:6 * k + 2], st6[:, u, :]).then_inc(ud, 1)
                    dv.wait_ge(ud, b + 2)
                    dv.tensor_scalar(tiny[:, u, 6 * k + 2:6 * k + 3], tiny[:, u, 6 * k + 1:6 * k + 2], EPS, None,
                                     ALU.add).then_inc(ve_done, 1)
                    dv.wait_ge(sq_done, 2 * t + k + 1)
                    dv.reciprocal(tiny[:, u, 6 * k + 3:6 * k + 4], tiny[:, u, 6 * k + 2:6 * k + 3]).then_inc(ud, 1)
                    dv.wait_ge(ud, b + 3)

                dv.wait_ge(gelu_done, t + 1)
                dv.tensor_tensor(sc[:, u, :], xs[:, u, :], sc[:, u, :], ALU.add).then_inc(ud, 1)
                dv.wait_ge(ud, base + 1)
                norm_stats(sc[:, u, :], 0, base + 1)
                dv.scalar_tensor_tensor(sc[:, u, :], sc[:, u, :], tiny[:, u, 0:1], gamma_b[:, :], ALU.subtract,
                                        ALU.mult).then_inc(ud, 1)
                dv.wait_ge(ud, base + 5)
                wait(dv, xb_done, NT)
                gate(dv, v_gate)
                dv.scalar_tensor_tensor(xs[:, u, :], sc[:, u, :], tiny[:, u, 3:4], tile_of(x_sb, t), ALU.mult,
                                        ALU.add).then_inc(x1_done, 1)
                dv.wait_ge(x1_done, t + 1)
                gate(dv, v_gate)
                norm_stats(xs[:, u, :], 1, base + 5)
                dv.tensor_scalar(sc[:, u, :], xs[:, u, :], tiny[:, u, 6:7], tiny[:, u, 9:10], ALU.subtract, ALU.mult)\
                    .then_inc(xa_done, 1)

            front(0, 0)
            front(1, 1)
            back(0, 0, 1)
            with dv.Fori(1, NT // 2) as pair:
                for u in range(2):
                    front(2 * pair + u, u)
                    back(2 * pair + (u - 1), 1 - u, 1)
            back(NT - 1, (NT - 1) % 2, 0)

            dv.wait_ge(small_in, 16 * 9)
            dv.tensor_scalar(cw1[:, :], cw[:, :, 1:2].rearrange("p a b -> p (a b)"), 1.0, None, ALU.add).then_inc(cv, 1)
            dv.wait_ge(cv, 1)
            dv.wait_ge(xaT_sb, NT)
            dv.wait_ge(x1b_done, NT)
            for c in range(FC):
                dv.tensor_scalar(xcT[:, c, 0:N], xaT[:, c, :], cw1[:, c:c + 1], pb[:, c:c + 1], ALU.mult, ALU.add)\
                    .then_inc(cv, 1)
                dv.wait_ge(cv, 3 * c + 2)
                dv.scalar_tensor_tensor(xcT[:, c, 1:N], xaT[:, c, 0:N - 1], cw[:, c, 0:1], xcT[:, c, 1:N], ALU.mult,
                                        ALU.add).then_inc(cv, 1)
                dv.wait_ge(cv, 3 * c + 3)
                dv.scalar_tensor_tensor(xcT[:, c, 0:N - 1], xaT[:, c, 1:N], cw[:, c, 2:3], xcT[:, c, 0:N - 1],
                                        ALU.mult, ALU.add).then_inc(cv, 1)
                dv.wait_ge(cv, 3 * c + 4)
                dv.sem_inc(xc_done, 1)

            dv.wait_ge(vones, 2)
            for t in range(NT):
                dv.wait_ge(v_ps, t + 1)
                dv.tensor_tensor(v_sb[:, t, :].rearrange("p (h w) -> p h w", w=VW)[:, :, 0:HD],
                                 bank(6 + t % 2, D, TP).rearrange("p (h w) -> p h w", w=HD),
                                 vb_b[:, :].rearrange("p (h w) -> p h w", w=HD), ALU.add).then_inc(v_done, 1)

            def select_first(n, s):
                dv.wait_ge(s_sb, n + 1)
                wait(dv, m_done, n - 1)
                gate(dv, v_gate)
                dv.max(top[:, s, 0:8], sS[:, s, :]).then_inc(max1, 1)
                dv.wait_ge(max1, n + 1)
                wait(dv, p_done, n - 1)
                gate(dv, v_gate)
                dv.match_replace(rS[:, s, :], top[:, s, 0:8], sS[:, s, :], REMOVED).then_inc(rep1, 1)

            def select_rest(n, s):
                dv.wait_ge(rep1, n + 1)
                gate(dv, v_gate)
                dv.max(top[:, s, 8:16], rS[:, s, :]).then_inc(max2, 1)
                dv.wait_ge(max2, n + 1)
                gate(dv, v_gate)
                dv.match_replace(rS[:, s, :], top[:, s, 8:16], rS[:, s, :], REMOVED).then_inc(rep2, 1)

            def output(n, h, u):
                dv.wait_ge(o_ps, n + 1)
                dv.reciprocal(rinv[:, h % 2, :], ps[0:TP, 6 * BANK + HD:6 * BANK + VW]).then_inc(inv_done, 1)
                dv.wait_ge(inv_done, n + 1)
                dv.tensor_scalar(o_sb[:, u, h * HD:(h + 1) * HD], ps[0:TP, 6 * BANK:6 * BANK + HD],
                                 rinv[:, h % 2, :], None, ALU.mult)\
                    .then_inc(o_done, 1)

            def result(t, u):
                dv.wait_ge(y_ps, t + 1)
                wait(dv, y_out[u], 16 * ((t - u) // 2) if isinstance(t, int) else 8 * (t - u))
                gate(dv, v_gate)
                dv.tensor_tensor(res[:, u, :], bank(7, D, TP), tile_of(x_sb, t), ALU.add).then_inc(y_done, 1)

            def tile(t, u, first=False):
                for h in range(HEADS):
                    n = HEADS * t + h
                    select_first(n, h % 2)
                    if h == 2:
                        wait(dv, oT_ps, t - 1)
                    if h >= 2:
                        output(n - 2, h - 2, u)
                    elif not first:
                        output(n - 2, h + HEADS - 2, 1 - u)
                    select_rest(n, h % 2)
                    if h == 5 and not first:
                        result(t - 1, 1 - u)

            tile(0, 0, True)
            tile(1, 1)
            with dv.Fori(1, NT // 2) as pair:
                for u in range(2):
                    tile(2 * pair + u, u)
            last = HEADS * NT
            for k in (2, 1):
                output(last - k, HEADS - k, (NT - 1) % 2)
            result(NT - 1, (NT - 1) % 2)

        @block.tensor
        def _(pe):
            pe.sem_inc(sums, R)
            pe.wait_ge(consts, 3)
            pe.wait_ge(ixd, 1)
            pe.matmul(ps[0:PATH, 7 * BANK:7 * BANK + NB], ones[0:1, 0:PATH], dl_f[0:1, :], start=True, stop=True)\
                .then_inc(ixp, 1)
            pe.wait_ge(ixd, 4)
            pe.matmul(ps[0:1, 6 * BANK:6 * BANK + 1], fall[:, 0:1], ones[0:TP, 0:1], start=True, stop=True)\
                .then_inc(ixp, 1)
            pe.wait_ge(ixd, 6)
            pe.matmul(ps[0:1, 5 * BANK:5 * BANK + PATH], stepped[:, 0:1], ident[0:PATH, 0:PATH],
                      start=True, stop=True).then_inc(ixp, 1)
            pe.wait_ge(ixd, 9)

            n = 0

            def fresh():
                nonlocal n
                if n >= 4:
                    pe.wait_ge(wt_sb, n - 3)
                n += 1
                return 4 + (n - 1) % 4

            pe.wait_ge(small_in, 16 * 9)
            for j in range(4):
                pe.matmul(bank(fresh(), D, TP), ones[0:1, 0:TP], w2T[0:1, j, :], start=True, stop=True)\
                    .then_inc(wt_ps, 1)
            pe.wait_ge(wu_in, 16)
            wu_nat = natA[:, :, :].rearrange("p a n -> p (a n)").rearrange("p (c f) -> p c f", c=FC)
            for f in range(2 * FC):
                b = fresh()
                for o in range(FC):
                    ins = pe.transpose(ps[:, b * BANK + o * P:b * BANK + (o + 1) * P], wu_nat[:, o, f * P:(f + 1) * P],
                                       ident[:, :])
                ins.then_inc(wt_ps, 1)
            pe.wait_ge(wm_in, 16)
            for i in range(FC):
                b = fresh()
                pe.wait_ge(wt_sb, 12)
                for m in range(FC):
                    ins = pe.matmul(bank(b), natB[:, m, i * P:(i + 1) * P], wu2T[:, m, :], start=(m == 0),
                                    stop=(m == FC - 1))
                ins.then_inc(wt_ps, 1)
            b = fresh()
            for m in range(FC):
                ins = pe.matmul(ps[32:33, b * BANK:(b + 1) * BANK], bmc[:, m:m + 1], wu2T[:, m, :], start=(m == 0),
                                stop=(m == FC - 1))
            ins.then_inc(wt_ps, 1)

            def turn(nat, first):
                for f in range(FC):
                    b = fresh()
                    for o in range(FC):
                        ins = pe.transpose(ps[:, b * BANK + o * P:b * BANK + (o + 1) * P],
                                           nat[:, first + o, f * P:(f + 1) * P], ident[:, :])
                    ins.then_inc(wt_ps, 1)

            pe.wait_ge(wq_in, 16)
            turn(natA, 0)
            turn(natA, 4)
            pe.wait_ge(wq2_in, 16)
            turn(natB, 0)

            def sum_items(first, end):
                with pe.Fori(first, end, R) as i:
                    for r in range(R):
                        b = 2 * (r % 2)
                        pe.wait_ge(hot_done, i + (r + 1))
                        pe.wait_ge(adds, i + (r + 1))
                        pe.wait_ge(gather_done[r], 16 * G * (i // R) + 16 * G)
                        for g in range(G):
                            pe.matmul(ps[0:TP, b * BANK:(b + 1) * BANK], onehot[:, r, g, :],
                                      ring[:, r, g * D:(g + 1) * D], start=(g == 0), stop=(g == G - 1))
                            ins = pe.matmul(ps[0:TP, (b + 1) * BANK:(b + 1) * BANK + 1], onehot[:, r, g, :],
                                            ones[:, 0:1], start=(g == 0), stop=(g == G - 1))
                        ins.then_inc(sums, 1)

            sum_items(0, PATH)
            unsorted = pe.value_load(flag_i[0:1, 0:1], min_val=0, max_val=1)
            with pe.If(unsorted > 0):
                sum_items(PATH, ALL)
            pe.end_ifs()
            pe.wait_ge(agg_done, 1)
            pe.wait_ge(wo_in, 16)
            turn(natA, 0)
            pe.wait_ge(wt_sb, n)

            def front(t, u):
                pe.wait_ge(xs_done, t + 1)
                for c in range(FC):
                    ins = pe.transpose(ps[:, 4 * u * BANK + c * TP:4 * u * BANK + (c + 1) * TP],
                                       xs[:, u, c * P:(c + 1) * P], ident[0:TP, 0:TP])
                ins.then_inc(upT, 1)
                pe.wait_ge(sc_done, t + 1)
                wait(pe, xaT_sb, t - 1)
                pe.matmul(ps[32:33, (4 * u + 3) * BANK:(4 * u + 3) * BANK + TP], tiny[:, u, 13:14],
                          ident[0:TP, 0:TP], start=True, stop=True)
                for c in range(FC):
                    ins = pe.transpose(ps[:, (4 * u + 1) * BANK + c * TP:(4 * u + 1) * BANK + (c + 1) * TP],
                                       sc[:, u, c * P:(c + 1) * P], ident[0:TP, 0:TP])
                ins.then_inc(upT, 1)
                pe.wait_ge(ulT, 3 * t + 3)
                wait(pe, gelu_done, t - 1)
                psu = bank(4 * u + 2, D, TP)
                for c in range(2 * FC):
                    pe.matmul(psu, lT[:, u, c, :], w1T[:, c, :] if c < FC else w2T[:, c - FC, :], start=(c == 0),
                              stop=False)
                pe.matmul(psu, blhs[:, u, :], brhs[:, :], start=False, stop=True).then_inc(u_ps, 1)

            def back(t, u):
                pe.wait_ge(xa_done, t + 1)
                for c in range(FC):
                    ins = pe.transpose(ps[:, (4 * u + 3) * BANK + c * TP:(4 * u + 3) * BANK + (c + 1) * TP],
                                       sc[:, u, c * P:(c + 1) * P], ident[0:TP, 0:TP])
                ins.then_inc(xaT_ps, 1)

            front(0, 0)
            front(1, 1)
            back(0, 0)
            with pe.Fori(1, NT // 2) as pair:
                for u in range(2):
                    front(2 * pair + u, u)
                    back(2 * pair + (u - 1), 1 - u)
            back(NT - 1, (NT - 1) % 2)

            pieces = ((0, BANK), (BANK, 2 * BANK), (2 * BANK, N))
            pe.wait_ge(xaT_sb, NT)
            for c in range(FC):
                b = 3 * (c % 2)
                if c >= 2:
                    pe.wait_ge(k_sb, c - 1)
                for f in range(FC):
                    pe.wait_ge(xc_done, f + 1)
                    for a, z in pieces:
                        ins = pe.matmul(ps[:, b * BANK + a:b * BANK + z], wqkvT[:, f, D + c * P:D + (c + 1) * P],
                                        xcT[:, f, a:z], start=(f == 0), stop=(f == FC - 1))
                ins.then_inc(k_ps, 1)
            for t in range(NT):
                if t >= 2:
                    pe.wait_ge(v_done, t - 1)
                for f in range(FC):
                    ins = pe.matmul(bank(6 + t % 2, D, TP), xcT[:, f, t * TP:(t + 1) * TP], wqkvT[:, f, 2 * D:3 * D],
                                    start=(f == 0), stop=(f == FC - 1))
                ins.then_inc(v_ps, 1)

            def queries(t):
                wait(pe, y_done, t - 1)
                for c in range(FC):
                    for f in range(FC):
                        rhs = xcT[:, f, t * TP:(t + 1) * TP] if isinstance(t, int) else xcT[:, f, bass.ds(t * TP, TP)]
                        ins = pe.matmul(ps[:, 7 * BANK + c * TP:7 * BANK + (c + 1) * TP],
                                        wqkvT[:, f, c * P:(c + 1) * P], rhs, start=(f == 0), stop=(f == FC - 1))
                ins.then_inc(q_ps, 1)

            def logits(n, t, h, u):
                if h == 0:
                    pe.wait_ge(q_sb, t + 1)
                wait(pe, s_sb, n)
                c, o = h // 2, HD * (h % 2)
                for a, z in pieces:
                    ins = pe.matmul(ps[0:TP, a:z], qcur[o:o + HD, u, c, :], kT[o:o + HD, c, a:z], start=True, stop=True)
                ins.then_inc(s_ps, 1)

            def values(n, h, s):
                pe.wait_ge(p_done, n + 1)
                for g, (a, b) in enumerate(((0, 4), (4, 8), (8, NT))):
                    wait(pe, pT_sb, 3 * (n - 1) + g + 1)
                    for k in range(a, b):
                        ins = pe.transpose(ps[0:TP, (3 + g) * BANK + (k - a) * TP:(3 + g) * BANK + (k - a + 1) * TP],
                                           eS[:, s, k * TP:(k + 1) * TP], ident[0:TP, 0:TP])
                    ins.then_inc(pT_ps, 1)
                wait(pe, o_done, n)
                for g, (a, b) in enumerate(((0, 4), (4, 8), (8, NT))):
                    pe.wait_ge(pT_sb, 3 * n + g + 1)
                    for k in range(a, b):
                        ins = pe.matmul(ps[0:TP, 6 * BANK:6 * BANK + VW], pT[:, s, k, :],
                                        v_sb[:, k, h * VW:(h + 1) * VW], start=(k == 0), stop=(k == NT - 1))
                ins.then_inc(o_ps, 1)

            def outT(t, u):
                pe.wait_ge(o_done, HEADS * (t + 1))
                for c in range(FC):
                    ins = pe.transpose(ps[:, 7 * BANK + c * TP:7 * BANK + (c + 1) * TP], o_sb[:, u, c * P:(c + 1) * P],
                                       ident[0:TP, 0:TP])
                ins.then_inc(oT_ps, 1)

            def project(t, u):
                pe.wait_ge(oT_sb, t + 1)
                for c in range(FC):
                    ins = pe.matmul(bank(7, D, TP), oT[:, u, c, :], woT[:, c, :], start=(c == 0), stop=(c == FC - 1))
                ins.then_inc(y_ps, 1)

            def tile(t, u, first=False):
                for h in range(HEADS):
                    n = HEADS * t + h
                    if h < HEADS - 1:
                        logits(n + 1, t, h + 1, u)
                    else:
                        logits(n + 1, t + 1, 0, 1 - u)
                    if not (first and h == 0):
                        values(n - 1, (h - 1) % HEADS, 1 - h % 2)
                    if h == 2 and not first:
                        outT(t - 1, 1 - u)
                    if h == 3 and not first:
                        project(t - 1, 1 - u)
                    if h == 6:
                        queries(t + 1)

            pe.wait_ge(vones, 2)
            pe.wait_ge(v_done, NT)
            queries(0)
            pe.wait_ge(k_sb, FC)
            logits(0, 0, 0, 0)
            tile(0, 0, True)
            tile(1, 1)
            with pe.Fori(1, NT // 2) as pair:
                for u in range(2):
                    tile(2 * pair + u, u)
            values(HEADS * NT - 1, HEADS - 1, 1)
            outT(NT - 1, (NT - 1) % 2)
            project(NT - 1, (NT - 1) % 2)


_INS = ["x", "src", "dst", "edge_attr_512", "L0_gnn_Wm", "L0_gnn_bm", "L0_gnn_Wu", "L0_gnn_bu", "L0_gnn_gamma",
        "L0_gnn_beta", "L0_ffn_pos_w", "L0_ffn_pos_b", "L0_ffn_qkv_w", "L0_ffn_qkv_b", "L0_ffn_wo_w", "L0_ffn_wo_b"]


def kernel(**inputs):
    import numpy as np
    from concourse import bacc
    from concourse.bass_utils import run_bass_kernel_spmd

    nc = bacc.Bacc("TRN2", target_bir_lowering=False, num_devices=1)
    arrays, args = {}, []
    for name in _INS:
        a = np.ascontiguousarray(inputs[name])
        arrays[f"in_{name}"] = a
        args.append(nc.dram_tensor(f"in_{name}", a.shape, mybir.dt.from_np(a.dtype), kind="ExternalInput").ap())
    out = nc.dram_tensor("out_x", (1250, 512), F32, kind="ExternalOutput").ap()
    gnn_ffn(nc, *args, out)
    r = run_bass_kernel_spmd(nc, [arrays], core_ids=[0])
    return r.results[0]["out_x"]
```

```python
from contextlib import ExitStack

import concourse.bass as bass
from concourse import mybir

F32 = mybir.dt.float32
F16 = mybir.dt.float16
F32R = mybir.dt.float32r
I32 = mybir.dt.int32
U32 = mybir.dt.uint32
ALU = mybir.AluOpType
ACT = mybir.ActivationFunctionType
AX = mybir.AxisListType

P = 128
BANK = 512
EPS = 1e-5
REMOVED = -3.0e38


def gnn_ffn(nc, x, src, dst, edge, Wm, bm, Wu, bu, gamma, beta, pos_w, pos_b, qkv_w, qkv_b, wo_w, wo_b, out):
    N, D = x.shape
    E = edge.shape[0]
    TP = 125
    NT = N // TP
    FC = D // P
    HEADS, HD = 8, 64
    G = 2
    BE = G * P
    NB = -(-E // BE)
    LAST = E - BE
    SEEN = (NB - 1) * BE - LAST
    R = 4
    PATH = 88
    ALL = 792
    TAB = 800
    SCALE = float(D) ** -0.5
    VW = HD + 1
    assert NT * TP == N and D == FC * P and SEEN % G == 0
    assert PATH >= NB + NT - 1 and PATH % R == 0 and ALL >= NB * NT and (ALL - PATH) % R == 0

    x_v = x.rearrange("(t p) d -> p t d", p=TP)
    out_v = out.rearrange("(t p) d -> t p d", p=TP)
    xn_d = nc.dram_tensor("xn_rows", (N, D), F32).ap()
    xn_v = xn_d.rearrange("(t p) d -> p t d", p=TP)
    row = lambda v: v.rearrange("(a d) -> a d", a=1)
    col = lambda v: v.rearrange("(c p) -> p c", p=P)

    def tile_of(ap, t):
        if isinstance(t, int):
            return ap[:, t, :]
        return ap[:, bass.ds(t, 1), :].rearrange("p a d -> p (a d)")

    def wait(eng, sem, value):
        if not (isinstance(value, int) and value <= 0):
            eng.wait_ge(sem, value)

    with ExitStack() as whole:
        def sem(name):
            return whole.enter_context(nc.semaphore(name))

        def sb(name, shape, dt=F32, stack=whole):
            return stack.enter_context(nc.sbuf_tensor(name, shape, dt))

        ps = whole.enter_context(nc.psum_tensor("ps", [P, 8 * BANK], F32))

        def bank(b, n=BANK, parts=P):
            return ps[0:parts, b * BANK:b * BANK + n]

        x_sb = sb("x_sb", [TP, NT, D])
        wqT = sb("wqT", [P, FC, D])
        wkvT = sb("wkvT", [P, FC, 2 * D])
        woT = sb("woT", [P, FC, D])
        xaT = sb("xaT", [P, FC, N])
        wu2T = xaT[:, :, :].rearrange("p c n -> p (c n)")[:, 0:FC * D].rearrange("p (c n) -> p c n", c=FC)
        gamma_b = sb("gamma_b", [TP, D])
        beta_b = sb("beta_b", [TP, D])
        late = sb("late", [P, 2, D])
        wob_b, vb_b = late[0:TP, 0, :], late[0:TP, 1, :]
        ident = sb("ident", [P, P])
        ones = sb("ones", [P, P])
        kb = sb("kb", [P, FC])
        cw = sb("cw", [P, FC, 3])
        cw1 = sb("cw1", [P, FC])
        pb = sb("pb", [P, FC])
        bmc = sb("bmc", [P, FC])
        brhs = sb("brhs", [33, D])

        gnn = ExitStack()
        g_sb = lambda n, s, d=F32: sb(n, s, d, gnn)
        xn = g_sb("xn", [TP, NT, D])
        acc = g_sb("acc", [TP, NT, D + 1])
        w1T = g_sb("w1T", [P, FC, D])
        w2T = g_sb("w2T", [P, FC, D])
        natA = g_sb("natA", [P, 8, D])
        natB = g_sb("natB", [P, 4, D])
        ring = g_sb("ring", [P, R, G * D])
        onehot = g_sb("onehot", [P, R, G, TP])
        iota_n = g_sb("iota_n", [P, NT, TP], F16)
        tab_b = g_sb("tab_b", [1, TAB], I32)
        tab_e = g_sb("tab_e", [1, TAB], I32)
        tab_t = g_sb("tab_t", [1, TAB], I32)
        dst_i = g_sb("dst_i", [P, NB + 1, G], I32)
        dst_f = g_sb("dst_f", [P, NB + 1, G])
        src_i = g_sb("src_i", [P, NB + 1, G], I32)
        idx = g_sb("idx", [P, R, G], I32)
        seq_a = g_sb("seq_a", [TP, E // TP], I32)
        seq_b = g_sb("seq_b", [TP, E // TP], I32)
        falls = g_sb("falls", [TP, E // TP])
        fall = g_sb("fall", [TP, 1])
        dl_i = g_sb("dl_i", [1, NB], I32)
        dl_f = g_sb("dl_f", [1, NB])
        thr = g_sb("thr", [PATH, NB])
        below = g_sb("below", [PATH, NB])
        stepped = g_sb("stepped", [PATH, 1])
        rows = g_sb("rows", [1, 6, PATH])
        flag_f = g_sb("flag_f", [1, 1])
        flag_i = g_sb("flag_i", [1, 1], I32)
        mv = g_sb("mv", [TP, NT, 2])
        st6 = g_sb("st6", [TP, NT, 6])
        sd = g_sb("sd", [TP, NT])
        rs = g_sb("rs", [TP, NT])
        xs = natA[0:TP, 4:6, :]
        sc = natA[0:TP, 6:8, :]
        lT = natB[:, :, :].rearrange("p a n -> p (a n)")[:, 0:4 * FC * TP]\
            .rearrange("p (u c n) -> p u c n", u=2, c=2 * FC)
        blhs = g_sb("blhs", [33, 2, TP])
        tiny = g_sb("tiny", [TP, 2, 16])
        gnn.close()

        ffn = ExitStack()
        f_sb = lambda n, s, d=F32: sb(n, s, d, ffn)
        xcT = f_sb("xcT", [P, FC, N + TP])
        k_parts = f_sb("k_parts", [P, HEADS, N], F32R)
        q_parts = f_sb("q_parts", [P, 2, 2, HEADS, TP], F32R)
        v_sb = f_sb("v_sb", [TP, NT, HEADS * VW])
        spare = wkvT[0:TP, :, :].rearrange("p c n -> p (c n)")
        eS = spare[:, 0:2 * N].rearrange("p (s n) -> p s n", s=2)
        o_sb = spare[:, 2 * N:2 * N + 2 * D].rearrange("p (s n) -> p s n", s=2)
        k_low = f_sb("k_low", [P, 4, N])
        rS = k_low[0:TP, :, :]
        pT = f_sb("pT", [TP, NT, TP])
        oT = late[:, :, 0:FC * TP].rearrange("p u (c n) -> p u c n", c=FC)
        res = (gamma_b, beta_b)
        top = f_sb("top", [TP, 2, 16])
        rinv = f_sb("rinv", [TP, 2, 1])
        negm = f_sb("negm", [TP, 2, 1])
        sS = xaT[0:TP, :, :].rearrange("p c n -> p (c n)")[:, 0:2 * N].rearrange("p (s n) -> p s n", s=2)
        ffn.close()

        x_in = [sem(f"x_in{i}") for i in range(2)]
        idx_in = sem("idx_in")
        small_in = sem("small_in")
        wu_in = sem("wu_in")
        wm_in = sem("wm_in")
        wq_in = sem("wq_in")
        wq2_in = sem("wq2_in")
        wo_in = sem("wo_in")
        xn_out = sem("xn_out")
        consts = sem("consts")
        padded = sem("padded")
        seqpad = sem("seqpad")
        ixd = sem("ixd")
        ixp = sem("ixp")
        tabs = sem("tabs")
        st_d = sem("st_d")
        sd_done = sem("sd_done")
        xn_done = sem("xn_done")
        xb_done = sem("xb_done")
        wt_ps = sem("wt_ps")
        wt_sb = sem("wt_sb")
        sums = sem("sums")
        load_done = [sem(f"load_done{i}") for i in range(R)]
        gather_done = [sem(f"gather_done{i}") for i in range(R)]
        idx_done = sem("idx_done")
        hot_done = sem("hot_done")
        adds = sem("adds")
        agg_done = sem("agg_done")
        p_gate, v_gate, a_gate, t_gate = sem("p_gate"), sem("v_gate"), sem("a_gate"), sem("t_gate")
        xs_done = sem("xs_done")
        sc_done = sem("sc_done")
        ud = sem("ud")
        upT = sem("upT")
        ulT = sem("ulT")
        u_ps = sem("u_ps")
        gelu_done = sem("gelu_done")
        ve_done = sem("ve_done")
        sq_done = sem("sq_done")
        x1_done = sem("x1_done")
        x1b_done = sem("x1b_done")
        xa_done = sem("xa_done")
        xaT_ps = sem("xaT_ps")
        xaT_sb = sem("xaT_sb")
        cv = sem("cv")
        xc_done = sem("xc_done")
        vones = sem("vones")
        k_ps = sem("k_ps")
        k_high = sem("k_high")
        k_lows = sem("k_lows")
        k_moved = [sem("k_moved0"), sem("k_moved1")]
        qb_in = sem("qb_in")
        v_ps = sem("v_ps")
        v_done = sem("v_done")
        q_ps = sem("q_ps")
        q_high = sem("q_high")
        q_low = sem("q_low")
        q_moved = [sem("q_moved0"), sem("q_moved1")]
        s_ps = sem("s_ps")
        s_sb = sem("s_sb")
        max1 = sem("max1")
        rep1 = sem("rep1")
        max2 = sem("max2")
        rep2 = sem("rep2")
        m_done = sem("m_done")
        e_done = sem("e_done")
        r_done = sem("r_done")
        p_done = sem("p_done")
        pT_ps = sem("pT_ps")
        pT_sb = sem("pT_sb")
        o_ps = sem("o_ps")
        inv_done = sem("inv_done")
        o_done = sem("o_done")
        oT_ps = sem("oT_ps")
        oT_sb = sem("oT_sb")
        y_ps = sem("y_ps")
        y_done = sem("y_done")
        y_out = [sem("y_out0"), sem("y_out1")]

        def gate(eng, s):
            eng.sem_inc(s, 1)

        EPN = E // TP
        block = whole.enter_context(nc.Block())

        @block.sync
        def _(sp):
            for h in range(2):
                t0, t1 = h * NT // 2, (h + 1) * NT // 2
                for a, b in ((0, 120), (120, TP)):
                    sp.dma_start(x_sb[a:b, t0:t1, :], x_v[a:b, t0:t1, :]).then_inc(x_in[h], 16)
            sp.dma_start(natA[:, 0:8, :].rearrange("p a n -> p (a n)").rearrange("p (c f) -> p c f", c=FC),
                         Wu.rearrange("(c p) f -> p c f", p=P)).then_inc(wu_in, 16)
            sp.dma_start(natB[:, :, :], Wm.rearrange("(c p) f -> p c f", p=P)).then_inc(wm_in, 16)
            sp.wait_ge(xn_done, NT)
            for a, b in ((0, 120), (120, TP)):
                sp.dma_start(xn_v[a:b, :, :], xn[a:b, :, :]).then_inc(xn_out, 16)
            sp.wait_ge(tabs, 1)

            def load_items(first, end):
                with sp.Fori(first, end, R) as i:
                    for r in range(R):
                        e0 = sp.value_load(tab_e[0:1, bass.ds(i + r, 1)], min_val=0, max_val=LAST)
                        sp.wait_ge(sums, i + (r + 1))
                        sp.dma_start(ring[:, r, :], edge[bass.ds(e0, BE), :].rearrange("(p g) d -> p (g d)", g=G))\
                            .then_inc(load_done[r], 16)

            load_items(0, PATH)
            unsorted = sp.value_load(flag_i[0:1, 0:1], min_val=0, max_val=1)
            with sp.If(unsorted > 0):
                load_items(PATH, ALL)
            sp.end_ifs()

            for c in range(FC):
                sp.wait_ge(k_lows, 2 * c + 2)
                for o in range(2):
                    sp.dma_start(k_parts[HD - HD * o:P - HD * o, 2 * c + o, :].bitcast(F32),
                                 k_low[HD * o:HD * o + HD, c % 2, :]).then_inc(k_moved[c % 2], 16)

            def spread_q(t, u):
                sp.wait_ge(q_low, 2 * t + 2)
                for o in range(2):
                    for part in range(2):
                        sp.dma_start(q_parts[HD - HD * o:P - HD * o, u, part, o:HEADS:2, :].bitcast(F32),
                                     q_parts[HD * o:HD * o + HD, u, part, o:HEADS:2, :].bitcast(F32))\
                            .then_inc(q_moved[u], 16)

            def store(t, u):
                sp.wait_ge(y_done, t + 1)
                dst_rows = out_v[t] if isinstance(t, int) else out_v[bass.ds(t, 1)].rearrange("a p d -> (a p) d")
                sp.dma_start(dst_rows, res[u][:, :]).then_inc(y_out[u], 16)

            spread_q(0, 0)
            spread_q(1, 1)
            with sp.Fori(1, NT // 2) as pair:
                for u in range(2):
                    spread_q(2 * pair + u, u)
                    store(2 * pair + (u - 2), u)
            spread_q(NT, 0)
            store(NT - 2, 0)
            store(NT - 1, 1)
            for u in range(2):
                sp.wait_ge(y_out[u], 16 * NT // 2)
            sp.wait_ge(q_moved[0], 64 * (NT // 2 + 1))

        @block.gpsimd
        def _(pl):
            pl.memset(ident[:, :], 0.0).then_inc(consts, 1)
            pl.memset(ones[:, :], 1.0).then_inc(consts, 1)
            pl.memset(seq_b[:, :], 1 << 20).then_inc(seqpad, 1)
            pl.wait_ge(consts, 1)
            pl.affine_select(out=ident[:, :], in_=ident[:, :], compare_op=ALU.not_equal, fill=1.0, base=0,
                             pattern=[[-1, P]], channel_multiplier=1).then_inc(consts, 1)
            pl.iota(thr[:, :], pattern=[[-TP, NB]], base=0, channel_multiplier=TP,
                    allow_small_or_imprecise_dtypes=True).then_inc(consts, 1)
            pl.iota(tab_b[0:1, :], pattern=[[1, TAB // NT], [0, NT]], base=0, channel_multiplier=0).then_inc(consts, 1)
            pl.iota(tab_t[0:1, :], pattern=[[0, TAB // NT], [1, NT]], base=0, channel_multiplier=0).then_inc(consts, 1)
            pl.iota(rows[0:1, 0, :], pattern=[[1, PATH]], base=0, channel_multiplier=0,
                    allow_small_or_imprecise_dtypes=True).then_inc(consts, 1)
            pl.iota(iota_n[:, :, :], pattern=[[TP, NT], [1, TP]], base=0, channel_multiplier=0,
                    allow_small_or_imprecise_dtypes=True).then_inc(consts, 1)
            pl.memset(blhs[:, :, :], 0.0).then_inc(consts, 1)
            pl.memset(brhs[:, :], 0.0).then_inc(consts, 1)
            pl.wait_ge(consts, 10)
            pl.memset(blhs[0:1, :, :], 1.0).then_inc(consts, 1)
            pl.wait_ge(idx_in, 16 * 9)
            pl.wait_ge(ixd, 2)
            pl.affine_select(out=dst_f[:, NB - 1, :], in_=dst_f[:, NB - 1, :], compare_op=ALU.is_ge, fill=-1.0,
                             base=-(SEEN // G), pattern=[[0, G]], channel_multiplier=1).then_inc(padded, 1)
            pl.memset(dst_f[:, NB, :], -1.0).then_inc(padded, 1)
            pl.tensor_copy(src_i[:, NB, :], src_i[:, NB - 1, :]).then_inc(padded, 1)
            pl.wait_ge(padded, 3)
            pl.wait_ge(tabs, 1)
            pl.wait_ge(xn_out, 32)

            def gather_items(first, end):
                with pl.Fori(first, end, R) as i:
                    for r in range(R):
                        b = pl.value_load(tab_b[0:1, bass.ds(i + r, 1)], min_val=0, max_val=NB)
                        pl.wait_ge(load_done[r], 16 * (i // R) + 16)
                        pl.tensor_copy(idx[:, r, :], tile_of(src_i, b)).then_inc(idx_done, 1)
                        pl.wait_ge(idx_done, i + (r + 1))
                        gate(pl, p_gate)
                        for g in range(G):
                            pl.indirect_dma_start(ring[:, r, g * D:(g + 1) * D], None, xn_d[:, :],
                                                  bass.IndirectOffsetOnAxis(ap=idx[:, r, g:g + 1].bitcast(U32), axis=0),
                                                  compute_op=ALU.add).then_inc(gather_done[r], 16)

            gather_items(0, PATH)
            unsorted = pl.value_load(flag_i[0:1, 0:1], min_val=0, max_val=1)
            with pl.If(unsorted > 0):
                gather_items(PATH, ALL)
            pl.end_ifs()
            pl.wait_ge(wt_sb, 4)
            for t in range(NT):
                pl.tensor_tensor(x_sb[:, t, :], x_sb[:, t, :], beta_b[:, :], ALU.add).then_inc(xb_done, 1)

            def keep_x1(t, u):
                pl.wait_ge(x1_done, t + 1)
                gate(pl, p_gate)
                pl.tensor_tensor(tile_of(x_sb, t), xs[:, u, :], wob_b, ALU.add).then_inc(x1b_done, 1)

            with pl.Fori(0, NT // 2) as pair:
                for u in range(2):
                    keep_x1(2 * pair + u, u)
            pl.wait_ge(xaT_sb, NT)
            pl.wait_ge(x1b_done, NT)
            pl.memset(v_sb[:, :, :], 1.0).then_inc(vones, 1)
            pl.memset(xcT[:, :, N:N + TP], 0.0).then_inc(vones, 1)

            def weights(n, s, r):
                pl.wait_ge(e_done, n + 1)
                pl.wait_ge(r_done, n + 1)
                gate(pl, p_gate)
                pl.tensor_tensor(eS[:, s, :], eS[:, s, :], rS[:, r, :], ALU.subtract).then_inc(p_done, 1)

            with pl.Fori(0, NT * HEADS, 4) as n:
                for r in range(4):
                    weights(n + r, r % 2, r)

        @block.scalar
        def _(act):
            row_in = lambda o, i: act.dma_start(o, i).then_inc(small_in, 16)
            act.wait_ge(seqpad, 1)
            ix = lambda o, i: act.dma_start(o, i, allow_slow_non_contiguous=True).then_inc(idx_in, 16)
            ix(seq_a[:, :], dst.rearrange("(p n) -> p n", p=TP))
            ix(seq_b[0:TP - 1, :], dst[1:1 + (TP - 1) * EPN].rearrange("(p n) -> p n", n=EPN))
            ix(seq_b[TP - 1:TP, 0:EPN - 1], row(dst[1 + (TP - 1) * EPN:E]))
            ix(dl_i[0:1, 0:NB - 1], dst[0:(NB - 1) * BE].rearrange("(a b) -> b a", b=BE)[BE - 1:BE, :])
            ix(dl_i[0:1, NB - 1:NB], row(dst[E - 1:E]))
            for tab, v in ((dst_i, dst), (src_i, src)):
                ix(tab[:, 0:NB - 1, :], v[0:(NB - 1) * BE].rearrange("(b p g) -> p b g", p=P, g=G))
                ix(tab[:, NB - 1, :], v[LAST:E].rearrange("(p g) -> p g", g=G))
            slow = lambda o, i: act.dma_start(o, i, allow_slow_non_contiguous=True).then_inc(small_in, 16)
            for j, v in enumerate((gamma, beta, wo_b, qkv_b[2 * D:3 * D])):
                row_in(w2T[0:1, j, :], row(v))
            act.wait_ge(consts, 11)
            row_in(brhs[0:1, :], row(bu))
            slow(kb[:, :], col(qkv_b[D:2 * D]))
            slow(bmc[:, :], col(bm))
            slow(pb[:, :], col(pos_b))
            slow(cw[:, :, :], pos_w.rearrange("(c p) a k -> p c (a k)", p=P))
            act.wait_ge(small_in, 16 * 9)
            act.wait_ge(st_d, 2 * NT + 1)
            act.activation(sd[:, :], sd[:, :], ACT.Sqrt).then_inc(sd_done, 1)

            n = 0

            def evac(dst_ap, src_ap):
                nonlocal n
                n += 1
                act.wait_ge(wt_ps, n)
                act.activation(dst_ap, src_ap, ACT.Copy).then_inc(wt_sb, 1)

            B4 = lambda n: 4 + n % 4
            for k, o in enumerate((gamma_b[:, :], beta_b[:, :], wob_b, vb_b)):
                evac(o, bank(B4(k), D, TP))
            for c in range(FC):
                evac(w1T[:, c, :], bank(B4(4 + c)))
            for c in range(FC):
                evac(wu2T[:, c, :], bank(B4(8 + c)))
            act.dma_start(natA[:, :, :], qkv_w[0:8 * P, :].rearrange("(c p) f -> p c f", p=P)).then_inc(wq_in, 16)
            for c in range(FC):
                evac(w2T[:, c, :], bank(B4(12 + c)))
            act.dma_start(natB[:, :, :], qkv_w[8 * P:12 * P, :].rearrange("(c p) f -> p c f", p=P)).then_inc(wq2_in, 16)
            evac(brhs[32:33, :], ps[32:33, 4 * BANK:5 * BANK])
            k = 17
            for j in range(3):
                for c in range(FC):
                    evac(wqT[:, c, :] if j == 0 else wkvT[:, c, (j - 1) * D:j * D], bank(B4(k)))
                    k += 1
                if j == 1:
                    act.dma_start(natA[:, 0:4, :], wo_w.rearrange("(c p) f -> p c f", p=P)).then_inc(wo_in, 16)
            for c in range(FC):
                evac(woT[:, c, :], bank(B4(k)))
                k += 1

            def front(t, u):
                wait(act, x1b_done, t - 1)
                wait(act, xa_done, t - 1)
                if not isinstance(t, int):
                    gate(act, a_gate)
                act.activation(xs[:, u, :], tile_of(xn, t), ACT.Copy).then_inc(xs_done, 1)
                act.wait_ge(upT, 2 * t + 1)
                wait(act, u_ps, t - 1)
                act.activation(lT[:, u, 0:FC, :].rearrange("p a b -> p (a b)"), bank(4 * u, FC * TP), ACT.Copy)\
                    .then_inc(ulT, 1)
                act.wait_ge(upT, 2 * t + 2)
                act.activation(lT[:, u, FC:2 * FC, :].rearrange("p a b -> p (a b)"), bank(4 * u + 1, FC * TP),
                               ACT.Copy).then_inc(ulT, 1)
                act.activation(blhs[32:33, u, :], ps[32:33, (4 * u + 3) * BANK:(4 * u + 3) * BANK + TP],
                               ACT.Copy).then_inc(ulT, 1)

            def back(t, u):
                act.wait_ge(u_ps, t + 1)
                act.activation(sc[:, u, :], bank(4 * u + 2, D, TP), ACT.Gelu).then_inc(gelu_done, 1)
                for k in range(2):
                    act.wait_ge(ve_done, 2 * t + k + 1)
                    act.activation(tiny[:, u, 2 + 6 * k:3 + 6 * k], tiny[:, u, 2 + 6 * k:3 + 6 * k], ACT.Sqrt)\
                        .then_inc(sq_done, 1)
                act.wait_ge(xaT_ps, t + 1)
                if not isinstance(t, int):
                    gate(act, a_gate)
                    dst_cols = xaT[:, :, bass.ds(t * TP, TP)]
                else:
                    dst_cols = xaT[:, :, t * TP:(t + 1) * TP]
                act.activation(dst_cols, bank(4 * u + 3, FC * TP).rearrange("p (c n) -> p c n", c=FC), ACT.Copy)\
                    .then_inc(xaT_sb, 1)

            front(0, 0)
            front(1, 1)
            back(0, 0)
            with act.Fori(1, NT // 2) as pair:
                for u in range(2):
                    front(2 * pair + u, u)
                    back(2 * pair + (u - 1), 1 - u)
            back(NT - 1, (NT - 1) % 2)

            act.wait_ge(u_ps, NT)
            act.dma_start(brhs[0:1, :], row(qkv_b[0:D])).then_inc(qb_in, 16)

            for c in range(FC):
                act.wait_ge(k_ps, c + 1)
                for o in range(2):
                    a, z = HD * o, HD * o + HD
                    act.activation(k_parts[a:z, 2 * c + o, :], ps[a:z, 3 * (c % 2) * BANK:3 * (c % 2) * BANK + N],
                                   ACT.Identity, bias=kb[a:z, c:c + 1]).then_inc(k_high, 1)

            def q_out(t, u):
                act.wait_ge(q_ps, t + 1)
                for o in range(2):
                    a, z = HD * o, HD * o + HD
                    act.activation(q_parts[a:z, u, 0, o:HEADS:2, :],
                                   ps[a:z, 7 * BANK:7 * BANK + FC * TP].rearrange("p (c n) -> p c n", c=FC),
                                   ACT.Copy, scale=SCALE).then_inc(q_high, 1)

            def copy_logits(n, s):
                act.wait_ge(s_ps, n + 1)
                wait(act, e_done, n - 1)
                wait(act, rep1, n - 1)
                act.activation(sS[:, s, :], ps[0:TP, 0:N], ACT.Copy).then_inc(s_sb, 1)

            def exp_logits(n, s):
                act.wait_ge(rep1, n + 1)
                wait(act, r_done, n - 1)
                act.mul(negm[:, s, :], top[:, s, 0:1], -1.0).then_inc(m_done, 1)
                act.wait_ge(m_done, n + 1)
                act.wait_ge(s_sb, n + 1)
                wait(act, pT_ps, 3 * (n - 1))
                act.activation(eS[:, s, :], sS[:, s, :], ACT.Exp, bias=negm[:, s, :]).then_inc(e_done, 1)

            def exp_rest(n, s):
                act.wait_ge(rep2, n + 1)
                act.activation(rS[:, s, :], rS[:, s, :], ACT.Exp, bias=negm[:, s % 2, :]).then_inc(r_done, 1)

            def weightsT(n):
                for g, (a, b) in enumerate(((0, 4), (4, 8), (8, NT))):
                    act.wait_ge(pT_ps, 3 * n + g + 1)
                    wait(act, o_ps, n)
                    act.activation(pT[:, a:b, :].rearrange("p a b -> p (a b)"),
                                   bank(3 + g, (b - a) * TP, TP), ACT.Copy).then_inc(pT_sb, 1)

            def outT(t, u):
                act.wait_ge(oT_ps, t + 1)
                wait(act, y_ps, t - 1)
                act.activation(oT[:, u, :, :].rearrange("p a b -> p (a b)"), bank(7, FC * TP), ACT.Copy)\
                    .then_inc(oT_sb, 1)

            def tile(t, u, first=False):
                for h in range(HEADS):
                    n = HEADS * t + h
                    if not (first and h < 2):
                        exp_rest(n - 2, (h - 2) % 4)
                    if h == 1:
                        q_out(t + 1, 1 - u)
                    if not (first and h < 3):
                        weightsT(n - 3)
                    if h == 5 and not first:
                        outT(t - 1, 1 - u)
                    if not (first and h < 1):
                        exp_logits(n - 1, 1 - h % 2)
                    copy_logits(n + 1, 1 - h % 2)

            q_out(0, 0)
            copy_logits(0, 0)
            tile(0, 0, True)
            tile(1, 1)
            with act.Fori(1, NT // 2) as pair:
                for u in range(2):
                    tile(2 * pair + u, u)
            last = HEADS * NT
            exp_rest(last - 2, 2)
            weightsT(last - 3)
            exp_logits(last - 1, 1)
            exp_rest(last - 1, 3)
            weightsT(last - 2)
            weightsT(last - 1)
            outT(NT - 1, (NT - 1) % 2)

        @block.vector
        def _(dv):
            dv.sem_inc(adds, 2)
            dv.wait_ge(idx_in, 16 * 9)
            dv.tensor_copy(dl_f[:, :], dl_i[:, :]).then_inc(ixd, 1)
            dv.tensor_copy(dst_f[:, 0:NB, :], dst_i[:, 0:NB, :]).then_inc(ixd, 1)
            dv.tensor_tensor(falls[:, :], seq_a[:, :], seq_b[:, :], ALU.is_gt).then_inc(ixd, 1)
            dv.wait_ge(ixd, 3)
            dv.tensor_reduce(fall[:, :], falls[:, :], AX.X, ALU.max).then_inc(ixd, 1)
            dv.wait_ge(ixp, 1)
            dv.wait_ge(consts, 7)
            dv.tensor_tensor(below[:, :], ps[0:PATH, 7 * BANK:7 * BANK + NB], thr[:, :], ALU.is_lt).then_inc(ixd, 1)
            dv.wait_ge(ixd, 5)
            dv.tensor_reduce(stepped[:, :], below[:, :], AX.X, ALU.add).then_inc(ixd, 1)
            dv.wait_ge(ixp, 2)
            dv.tensor_scalar(flag_f[:, :], ps[0:1, 6 * BANK:6 * BANK + 1], 1.0, None, ALU.min).then_inc(ixd, 1)
            dv.wait_ge(ixd, 7)
            dv.tensor_copy(flag_i[:, :], flag_f[:, :]).then_inc(ixd, 1)
            dv.wait_ge(ixp, 3)
            b_row, t_row, db, dt_, gb, gt = (rows[0:1, j, :] for j in (1, 2, 3, 4, 5, 5))
            dv.tensor_copy(b_row, ps[0:1, 5 * BANK:5 * BANK + PATH]).then_inc(ixd, 1)
            dv.wait_ge(ixd, 9)
            dv.tensor_tensor(t_row, rows[0:1, 0, :], b_row, ALU.subtract).then_inc(ixd, 1)
            dv.wait_ge(ixd, 10)
            dv.tensor_tensor(db, tab_b[0:1, 0:PATH], b_row, ALU.subtract).then_inc(ixd, 1)
            dv.tensor_tensor(dt_, tab_t[0:1, 0:PATH], t_row, ALU.subtract).then_inc(ixd, 1)
            dv.wait_ge(ixd, 12)
            dv.scalar_tensor_tensor(gb, db, flag_f[:, 0:1], b_row, ALU.mult, ALU.add).then_inc(ixd, 1)
            dv.wait_ge(ixd, 13)
            dv.tensor_copy(tab_b[0:1, 0:PATH], gb).then_inc(ixd, 1)
            dv.wait_ge(ixd, 14)
            dv.scalar_tensor_tensor(gt, dt_, flag_f[:, 0:1], t_row, ALU.mult, ALU.add).then_inc(ixd, 1)
            dv.wait_ge(ixd, 15)
            dv.tensor_scalar(tab_t[0:1, 0:PATH], gt, float(NT - 1), 0.0, ALU.min, ALU.max).then_inc(ixd, 1)
            dv.tensor_scalar(tab_e[0:1, :], tab_b[0:1, :], float(BE), float(LAST), ALU.mult, ALU.min).then_inc(ixd, 1)
            dv.wait_ge(ixd, 17)
            dv.memset(acc[:, :, :], 0.0).then_inc(tabs, 1)

            for t in range(NT):
                dv.wait_ge(x_in[t // (NT // 2)], 32)
                dv.bn_stats(st6[:, t, :], x_sb[:, t, :]).then_inc(st_d, 1)
            for t in range(NT):
                dv.wait_ge(st_d, t + 1)
                dv.bn_aggr(mv[:, t, :], st6[:, t, :]).then_inc(st_d, 1)
            dv.wait_ge(st_d, 2 * NT)
            dv.tensor_scalar(sd[:, :], mv[:, :, 1:2].rearrange("p a b -> p (a b)"), EPS, None, ALU.add)\
                .then_inc(st_d, 1)
            dv.wait_ge(sd_done, 1)
            dv.reciprocal(rs[:, :], sd[:, :]).then_inc(st_d, 1)
            dv.wait_ge(st_d, 2 * NT + 2)
            for t in range(NT):
                dv.tensor_scalar(xn[:, t, :], x_sb[:, t, :], mv[:, t, 0:1], rs[:, t:t + 1], ALU.subtract, ALU.mult)\
                    .then_inc(xn_done, 1)

            def hot(k, r, count):
                b = dv.value_load(tab_b[0:1, bass.ds(k, 1)], min_val=0, max_val=NB)
                j = dv.value_load(tab_t[0:1, bass.ds(k, 1)], min_val=0, max_val=NT - 1)
                wait(dv, sums, count)
                if not isinstance(count, int):
                    gate(dv, v_gate)
                for g in range(G):
                    ins = dv.tensor_scalar(onehot[:, r, g, :], tile_of(iota_n, j),
                                           dst_f[:, bass.ds(b, 1), g:g + 1].rearrange("p a b -> p (a b)"), None,
                                           ALU.is_equal)
                ins.then_inc(hot_done, 1)

            def add(k, r):
                j = dv.value_load(tab_t[0:1, bass.ds(k, 1)], min_val=0, max_val=NT - 1)
                dv.wait_ge(sums, k + (R + 1))
                dv.wait_ge(adds, k + 2)
                gate(dv, v_gate)
                dv.tensor_tensor(tile_of(acc, j), tile_of(acc, j), ps[0:TP, 2 * (r % 2) * BANK:2 * (r % 2) * BANK + D + 1],
                                 ALU.add).then_inc(adds, 1)

            def sum_items(first, end):
                with dv.Fori(first, end, R) as i:
                    for r in range(R):
                        hot(i + (r + 2), (r + 2) % R, i + (r + 3))
                        add(i + r, r)

            dv.wait_ge(padded, 3)
            dv.wait_ge(consts, 8)
            dv.wait_ge(tabs, 1)
            hot(0, 0, 0)
            hot(1, 1, 0)
            sum_items(0, PATH)
            dv.wait_ge(adds, PATH + 2)
            unsorted = dv.value_load(flag_i[0:1, 0:1], min_val=0, max_val=1)
            with dv.If(unsorted > 0):
                sum_items(PATH, ALL)
                dv.wait_ge(adds, ALL + 2)
            dv.end_ifs()
            dv.memset(tiny[:, :, :], 0.0).then_inc(agg_done, 1)
            dv.wait_ge(agg_done, 1)

            STEP = 11

            def front(t, u):
                cnt = tile_of(acc, t)[:, D:D + 1]
                base = 0 if isinstance(t, int) and t == 0 else STEP * t - (STEP - 3)
                wait(dv, xaT_ps, t - 1)
                if not isinstance(t, int):
                    gate(dv, v_gate)
                dv.tensor_scalar(tiny[:, u, 12:13], cnt, 1.0, None, ALU.max).then_inc(ud, 1)
                dv.tensor_scalar(tiny[:, u, 13:14], cnt, 1.0, None, ALU.min).then_inc(ud, 1)
                dv.wait_ge(ud, base + 2)
                dv.reciprocal(tiny[:, u, 14:15], tiny[:, u, 12:13]).then_inc(ud, 1)
                dv.wait_ge(ud, base + 3)
                gate(dv, v_gate)
                dv.tensor_scalar(sc[:, u, :], tile_of(acc, t)[:, 0:D], tiny[:, u, 14:15], None, ALU.mult)\
                    .then_inc(sc_done, 1)

            def back(t, u, ahead):
                base = STEP * t + 3 + ahead * 3

                def norm_stats(src_ap, k, b):
                    dv.bn_stats(st6[:, u, :], src_ap).then_inc(ud, 1)
                    dv.wait_ge(ud, b + 1)
                    gate(dv, v_gate)
                    dv.bn_aggr(tiny[:, u, 6 * k + 0:6 * k + 2], st6[:, u, :]).then_inc(ud, 1)
                    dv.wait_ge(ud, b + 2)
                    dv.tensor_scalar(tiny[:, u, 6 * k + 2:6 * k + 3], tiny[:, u, 6 * k + 1:6 * k + 2], EPS, None,
                                     ALU.add).then_inc(ve_done, 1)
                    dv.wait_ge(sq_done, 2 * t + k + 1)
                    dv.reciprocal(tiny[:, u, 6 * k + 3:6 * k + 4], tiny[:, u, 6 * k + 2:6 * k + 3]).then_inc(ud, 1)
                    dv.wait_ge(ud, b + 3)

                dv.wait_ge(gelu_done, t + 1)
                dv.tensor_tensor(sc[:, u, :], xs[:, u, :], sc[:, u, :], ALU.add).then_inc(ud, 1)
                dv.wait_ge(ud, base + 1)
                norm_stats(sc[:, u, :], 0, base + 1)
                dv.scalar_tensor_tensor(sc[:, u, :], sc[:, u, :], tiny[:, u, 0:1], gamma_b[:, :], ALU.subtract,
                                        ALU.mult).then_inc(ud, 1)
                dv.wait_ge(ud, base + 5)
                wait(dv, xb_done, NT)
                gate(dv, v_gate)
                dv.scalar_tensor_tensor(xs[:, u, :], sc[:, u, :], tiny[:, u, 3:4], tile_of(x_sb, t), ALU.mult,
                                        ALU.add).then_inc(x1_done, 1)
                dv.wait_ge(x1_done, t + 1)
                gate(dv, v_gate)
                norm_stats(xs[:, u, :], 1, base + 5)
                dv.tensor_scalar(sc[:, u, :], xs[:, u, :], tiny[:, u, 6:7], tiny[:, u, 9:10], ALU.subtract, ALU.mult)\
                    .then_inc(xa_done, 1)

            front(0, 0)
            front(1, 1)
            back(0, 0, 1)
            with dv.Fori(1, NT // 2) as pair:
                for u in range(2):
                    front(2 * pair + u, u)
                    back(2 * pair + (u - 1), 1 - u, 1)
            back(NT - 1, (NT - 1) % 2, 0)

            dv.wait_ge(small_in, 16 * 9)
            dv.tensor_scalar(cw1[:, :], cw[:, :, 1:2].rearrange("p a b -> p (a b)"), 1.0, None, ALU.add).then_inc(cv, 1)
            dv.wait_ge(cv, 1)
            dv.wait_ge(xaT_sb, NT)
            dv.wait_ge(x1b_done, NT)
            for c in range(FC):
                dv.tensor_scalar(xcT[:, c, 0:N], xaT[:, c, :], cw1[:, c:c + 1], pb[:, c:c + 1], ALU.mult, ALU.add)\
                    .then_inc(cv, 1)
                dv.wait_ge(cv, 3 * c + 2)
                dv.scalar_tensor_tensor(xcT[:, c, 1:N], xaT[:, c, 0:N - 1], cw[:, c, 0:1], xcT[:, c, 1:N], ALU.mult,
                                        ALU.add).then_inc(cv, 1)
                dv.wait_ge(cv, 3 * c + 3)
                dv.scalar_tensor_tensor(xcT[:, c, 0:N - 1], xaT[:, c, 1:N], cw[:, c, 2:3], xcT[:, c, 0:N - 1],
                                        ALU.mult, ALU.add).then_inc(cv, 1)
                dv.wait_ge(cv, 3 * c + 4)
                dv.sem_inc(xc_done, 1)

            for c in range(FC):
                if c >= 2:
                    dv.wait_ge(k_moved[c % 2], 32)
                dv.wait_ge(k_high, 2 * c + 2)
                for o in range(2):
                    a, z = HD * o, HD * o + HD
                    dv.scalar_tensor_tensor(k_low[a:z, c % 2, :].bitcast(F32R), ps[a:z, 3 * (c % 2) * BANK:3 * (c % 2) * BANK + N],
                                            kb[a:z, c:c + 1], k_parts[a:z, 2 * c + o, :].bitcast(F32), ALU.add,
                                            ALU.subtract).then_inc(k_lows, 1)

            dv.wait_ge(vones, 2)
            for t in range(NT):
                dv.wait_ge(v_ps, t + 1)
                dv.tensor_tensor(v_sb[:, t, :].rearrange("p (h w) -> p h w", w=VW)[:, :, 0:HD],
                                 bank(6 + t % 2, D, TP).rearrange("p (h w) -> p h w", w=HD),
                                 vb_b.rearrange("p (h w) -> p h w", w=HD), ALU.add).then_inc(v_done, 1)

            def q_rest(t, u):
                dv.wait_ge(q_high, 2 * t + 2)
                for o in range(2):
                    a, z = HD * o, HD * o + HD
                    dv.scalar_tensor_tensor(q_parts[a:z, u, 1, o:HEADS:2, :],
                                            ps[a:z, 7 * BANK:7 * BANK + FC * TP].rearrange("p (c n) -> p c n", c=FC),
                                            SCALE, q_parts[a:z, u, 0, o:HEADS:2, :].bitcast(F32), ALU.mult,
                                            ALU.subtract).then_inc(q_low, 1)

            def first_eight(n, s):
                dv.wait_ge(s_sb, n + 1)
                wait(dv, m_done, n - 1)
                gate(dv, v_gate)
                dv.max(top[:, s, 0:8], sS[:, s, :]).then_inc(max1, 1)

            def without_eight(n, s, r):
                dv.wait_ge(max1, n + 1)
                wait(dv, p_done, n - 3)
                gate(dv, v_gate)
                dv.match_replace(rS[:, r, :], top[:, s, 0:8], sS[:, s, :], REMOVED).then_inc(rep1, 1)

            def next_eight(n, s, r):
                dv.wait_ge(rep1, n + 1)
                gate(dv, v_gate)
                dv.max(top[:, s, 8:16], rS[:, r, :]).then_inc(max2, 1)

            def without_sixteen(n, s, r):
                dv.wait_ge(max2, n + 1)
                gate(dv, v_gate)
                dv.match_replace(rS[:, r, :], top[:, s, 8:16], rS[:, r, :], REMOVED).then_inc(rep2, 1)

            def invert(n, h):
                dv.wait_ge(o_ps, n + 1)
                dv.reciprocal(rinv[:, h % 2, :], ps[0:TP, 6 * BANK + HD:6 * BANK + VW]).then_inc(inv_done, 1)

            def output(n, h, u):
                dv.wait_ge(inv_done, n + 1)
                dv.tensor_scalar(o_sb[:, u, h * HD:(h + 1) * HD], ps[0:TP, 6 * BANK:6 * BANK + HD],
                                 rinv[:, h % 2, :], None, ALU.mult).then_inc(o_done, 1)

            def result(t, u):
                dv.wait_ge(y_ps, t + 1)
                wait(dv, y_out[u], 16 * ((t - u) // 2) if isinstance(t, int) else 8 * (t - u))
                gate(dv, v_gate)
                dv.tensor_tensor(res[u][:, :], bank(7, D, TP), tile_of(x_sb, t), ALU.add).then_inc(y_done, 1)

            def tile(t, u, first=False):
                for h in range(HEADS):
                    n = HEADS * t + h
                    old = not (first and h < 4)
                    if old:
                        invert(n - 4, h)
                    first_eight(n, h % 2)
                    if h == 4:
                        wait(dv, oT_ps, t - 1)
                    if old:
                        output(n - 4, (h - 4) % HEADS, u if h >= 4 else 1 - u)
                    if not (first and h < 1):
                        next_eight(n - 1, 1 - h % 2, (h - 1) % 4)
                    without_eight(n, h % 2, h % 4)
                    if not (first and h < 1):
                        without_sixteen(n - 1, 1 - h % 2, (h - 1) % 4)
                    if h == 1:
                        q_rest(t + 1, 1 - u)
                    if h == 7 and not first:
                        result(t - 1, 1 - u)

            q_rest(0, 0)
            tile(0, 0, True)
            tile(1, 1)
            with dv.Fori(1, NT // 2) as pair:
                for u in range(2):
                    tile(2 * pair + u, u)
            last = HEADS * NT
            next_eight(last - 1, 1, 3)
            without_sixteen(last - 1, 1, 3)
            for k in (4, 3, 2, 1):
                invert(last - k, HEADS - k)
                output(last - k, HEADS - k, (NT - 1) % 2)
            result(NT - 1, (NT - 1) % 2)

        @block.tensor
        def _(pe):
            pe.sem_inc(sums, R)
            pe.wait_ge(consts, 3)
            pe.wait_ge(ixd, 1)
            pe.matmul(ps[0:PATH, 7 * BANK:7 * BANK + NB], ones[0:1, 0:PATH], dl_f[0:1, :], start=True, stop=True)\
                .then_inc(ixp, 1)
            pe.wait_ge(ixd, 4)
            pe.matmul(ps[0:1, 6 * BANK:6 * BANK + 1], fall[:, 0:1], ones[0:TP, 0:1], start=True, stop=True)\
                .then_inc(ixp, 1)
            pe.wait_ge(ixd, 6)
            pe.matmul(ps[0:1, 5 * BANK:5 * BANK + PATH], stepped[:, 0:1], ident[0:PATH, 0:PATH],
                      start=True, stop=True).then_inc(ixp, 1)
            pe.wait_ge(ixd, 9)

            n = 0

            def fresh():
                nonlocal n
                if n >= 4:
                    pe.wait_ge(wt_sb, n - 3)
                n += 1
                return 4 + (n - 1) % 4

            pe.wait_ge(small_in, 16 * 9)
            for j in range(4):
                pe.matmul(bank(fresh(), D, TP), ones[0:1, 0:TP], w2T[0:1, j, :], start=True, stop=True)\
                    .then_inc(wt_ps, 1)
            pe.wait_ge(wu_in, 16)
            wu_nat = natA[:, :, :].rearrange("p a n -> p (a n)").rearrange("p (c f) -> p c f", c=FC)
            for f in range(2 * FC):
                b = fresh()
                for o in range(FC):
                    ins = pe.transpose(ps[:, b * BANK + o * P:b * BANK + (o + 1) * P], wu_nat[:, o, f * P:(f + 1) * P],
                                       ident[:, :])
                ins.then_inc(wt_ps, 1)
            pe.wait_ge(wm_in, 16)
            for i in range(FC):
                b = fresh()
                pe.wait_ge(wt_sb, 12)
                for m in range(FC):
                    ins = pe.matmul(bank(b), natB[:, m, i * P:(i + 1) * P], wu2T[:, m, :], start=(m == 0),
                                    stop=(m == FC - 1))
                ins.then_inc(wt_ps, 1)
            b = fresh()
            for m in range(FC):
                ins = pe.matmul(ps[32:33, b * BANK:(b + 1) * BANK], bmc[:, m:m + 1], wu2T[:, m, :], start=(m == 0),
                                stop=(m == FC - 1))
            ins.then_inc(wt_ps, 1)

            def turn(nat, first):
                for f in range(FC):
                    b = fresh()
                    for o in range(FC):
                        ins = pe.transpose(ps[:, b * BANK + o * P:b * BANK + (o + 1) * P],
                                           nat[:, first + o, f * P:(f + 1) * P], ident[:, :])
                    ins.then_inc(wt_ps, 1)

            pe.wait_ge(wq_in, 16)
            turn(natA, 0)
            turn(natA, 4)
            pe.wait_ge(wq2_in, 16)
            turn(natB, 0)

            def sum_items(first, end):
                with pe.Fori(first, end, R) as i:
                    for r in range(R):
                        b = 2 * (r % 2)
                        pe.wait_ge(hot_done, i + (r + 1))
                        pe.wait_ge(adds, i + (r + 1))
                        pe.wait_ge(gather_done[r], 16 * G * (i // R) + 16 * G)
                        for g in range(G):
                            pe.matmul(ps[0:TP, b * BANK:(b + 1) * BANK], onehot[:, r, g, :],
                                      ring[:, r, g * D:(g + 1) * D], start=(g == 0), stop=(g == G - 1))
                            ins = pe.matmul(ps[0:TP, (b + 1) * BANK:(b + 1) * BANK + 1], onehot[:, r, g, :],
                                            ones[:, 0:1], start=(g == 0), stop=(g == G - 1))
                        ins.then_inc(sums, 1)

            sum_items(0, PATH)
            unsorted = pe.value_load(flag_i[0:1, 0:1], min_val=0, max_val=1)
            with pe.If(unsorted > 0):
                sum_items(PATH, ALL)
            pe.end_ifs()
            pe.wait_ge(agg_done, 1)
            pe.wait_ge(wo_in, 16)
            turn(natA, 0)
            pe.wait_ge(wt_sb, n)

            def front(t, u):
                pe.wait_ge(xs_done, t + 1)
                for c in range(FC):
                    ins = pe.transpose(ps[:, 4 * u * BANK + c * TP:4 * u * BANK + (c + 1) * TP],
                                       xs[:, u, c * P:(c + 1) * P], ident[0:TP, 0:TP])
                ins.then_inc(upT, 1)
                pe.wait_ge(sc_done, t + 1)
                wait(pe, xaT_sb, t - 1)
                pe.matmul(ps[32:33, (4 * u + 3) * BANK:(4 * u + 3) * BANK + TP], tiny[:, u, 13:14],
                          ident[0:TP, 0:TP], start=True, stop=True)
                for c in range(FC):
                    ins = pe.transpose(ps[:, (4 * u + 1) * BANK + c * TP:(4 * u + 1) * BANK + (c + 1) * TP],
                                       sc[:, u, c * P:(c + 1) * P], ident[0:TP, 0:TP])
                ins.then_inc(upT, 1)
                pe.wait_ge(ulT, 3 * t + 3)
                wait(pe, gelu_done, t - 1)
                psu = bank(4 * u + 2, D, TP)
                for c in range(2 * FC):
                    pe.matmul(psu, lT[:, u, c, :], w1T[:, c, :] if c < FC else w2T[:, c - FC, :], start=(c == 0),
                              stop=False)
                pe.matmul(psu, blhs[:, u, :], brhs[:, :], start=False, stop=True).then_inc(u_ps, 1)

            def back(t, u):
                pe.wait_ge(xa_done, t + 1)
                for c in range(FC):
                    ins = pe.transpose(ps[:, (4 * u + 3) * BANK + c * TP:(4 * u + 3) * BANK + (c + 1) * TP],
                                       sc[:, u, c * P:(c + 1) * P], ident[0:TP, 0:TP])
                ins.then_inc(xaT_ps, 1)

            front(0, 0)
            front(1, 1)
            back(0, 0)
            with pe.Fori(1, NT // 2) as pair:
                for u in range(2):
                    front(2 * pair + u, u)
                    back(2 * pair + (u - 1), 1 - u)
            back(NT - 1, (NT - 1) % 2)

            pieces = ((0, BANK), (BANK, 2 * BANK), (2 * BANK, N))
            pe.wait_ge(xaT_sb, NT)
            for c in range(FC):
                b = 3 * (c % 2)
                if c >= 2:
                    pe.wait_ge(k_lows, 2 * (c - 1))
                for f in range(FC):
                    pe.wait_ge(xc_done, f + 1)
                    for a, z in pieces:
                        ins = pe.matmul(ps[:, b * BANK + a:b * BANK + z], wkvT[:, f, c * P:(c + 1) * P],
                                        xcT[:, f, a:z], start=(f == 0), stop=(f == FC - 1))
                ins.then_inc(k_ps, 1)
            for t in range(NT):
                if t >= 2:
                    pe.wait_ge(v_done, t - 1)
                for f in range(FC):
                    ins = pe.matmul(bank(6 + t % 2, D, TP), xcT[:, f, t * TP:(t + 1) * TP], wkvT[:, f, D:2 * D],
                                    start=(f == 0), stop=(f == FC - 1))
                ins.then_inc(v_ps, 1)

            def queries(t):
                wait(pe, y_done, t - 2)
                for c in range(FC):
                    for f in range(FC):
                        rhs = xcT[:, f, t * TP:(t + 1) * TP] if isinstance(t, int) else xcT[:, f, bass.ds(t * TP, TP)]
                        pe.matmul(ps[:, 7 * BANK + c * TP:7 * BANK + (c + 1) * TP],
                                  wqT[:, f, c * P:(c + 1) * P], rhs, start=(f == 0), stop=False)
                    ins = pe.matmul(ps[:, 7 * BANK + c * TP:7 * BANK + (c + 1) * TP], brhs[0:1, c * P:(c + 1) * P],
                                    ones[0:1, 0:TP], start=False, stop=True)
                ins.then_inc(q_ps, 1)

            def logits(n, t, h, u):
                if h == 0:
                    pe.wait_ge(q_moved[u], 64 * (t // 2 + 1) if isinstance(t, int) else 32 * (t - u) + 64)
                wait(pe, s_sb, n)
                for part in range(2):
                    for a, z in pieces:
                        ins = pe.matmul(ps[0:TP, a:z], q_parts[:, u, part, h, :], k_parts[:, h, a:z],
                                        start=(part == 0), stop=(part == 1))
                ins.then_inc(s_ps, 1)

            def turn_weights(n, s):
                pe.wait_ge(p_done, n + 1)
                for g, (a, b) in enumerate(((0, 4), (4, 8), (8, NT))):
                    wait(pe, pT_sb, 3 * (n - 1) + g + 1)
                    for k in range(a, b):
                        ins = pe.transpose(ps[0:TP, (3 + g) * BANK + (k - a) * TP:(3 + g) * BANK + (k - a + 1) * TP],
                                           eS[:, s, k * TP:(k + 1) * TP], ident[0:TP, 0:TP])
                    ins.then_inc(pT_ps, 1)

            def values(n, h):
                wait(pe, o_done, n)
                for g, (a, b) in enumerate(((0, 4), (4, 8), (8, NT))):
                    pe.wait_ge(pT_sb, 3 * n + g + 1)
                    for k in range(a, b):
                        ins = pe.matmul(ps[0:TP, 6 * BANK:6 * BANK + VW], pT[:, k, :],
                                        v_sb[:, k, h * VW:(h + 1) * VW], start=(k == 0), stop=(k == NT - 1))
                ins.then_inc(o_ps, 1)

            def outT(t, u):
                pe.wait_ge(o_done, HEADS * (t + 1))
                pe.wait_ge(q_low, 2 * (t + 2) + 2 if not isinstance(t, int) or t < NT - 1 else 2 * (NT + 1))
                for c in range(FC):
                    ins = pe.transpose(ps[:, 7 * BANK + c * TP:7 * BANK + (c + 1) * TP], o_sb[:, u, c * P:(c + 1) * P],
                                       ident[0:TP, 0:TP])
                ins.then_inc(oT_ps, 1)

            def project(t, u):
                pe.wait_ge(oT_sb, t + 1)
                for c in range(FC):
                    ins = pe.matmul(bank(7, D, TP), oT[:, u, c, :], woT[:, c, :], start=(c == 0), stop=(c == FC - 1))
                ins.then_inc(y_ps, 1)

            def tile(t, u, first=False):
                for h in range(HEADS):
                    n = HEADS * t + h
                    if not (first and h < 3):
                        turn_weights(n - 3, 1 - h % 2)
                    if h < HEADS - 1:
                        logits(n + 1, t, h + 1, u)
                    else:
                        logits(n + 1, t + 1, 0, 1 - u)
                    if not (first and h < 3):
                        values(n - 3, (h - 3) % HEADS)
                    if h == 0:
                        queries(t + 1)
                    if h == 4 and not first:
                        outT(t - 1, 1 - u)
                    if h == 5 and not first:
                        project(t - 1, 1 - u)

            pe.wait_ge(vones, 2)
            pe.wait_ge(v_done, NT)
            pe.wait_ge(qb_in, 16)
            queries(0)
            for moved in k_moved:
                pe.wait_ge(moved, 16 * FC)
            logits(0, 0, 0, 0)
            tile(0, 0, True)
            tile(1, 1)
            with pe.Fori(1, NT // 2) as pair:
                for u in range(2):
                    tile(2 * pair + u, u)
            for k in (3, 2, 1):
                turn_weights(HEADS * NT - k, k % 2)
                values(HEADS * NT - k, HEADS - k)
            outT(NT - 1, (NT - 1) % 2)
            project(NT - 1, (NT - 1) % 2)


_INS = ["x", "src", "dst", "edge_attr_512", "L0_gnn_Wm", "L0_gnn_bm", "L0_gnn_Wu", "L0_gnn_bu", "L0_gnn_gamma",
        "L0_gnn_beta", "L0_ffn_pos_w", "L0_ffn_pos_b", "L0_ffn_qkv_w", "L0_ffn_qkv_b", "L0_ffn_wo_w", "L0_ffn_wo_b"]


def kernel(**inputs):
    import numpy as np
    from concourse import bacc
    from concourse.bass_utils import run_bass_kernel_spmd

    nc = bacc.Bacc("TRN2", target_bir_lowering=False, num_devices=1)
    arrays, args = {}, []
    for name in _INS:
        a = np.ascontiguousarray(inputs[name])
        arrays[f"in_{name}"] = a
        args.append(nc.dram_tensor(f"in_{name}", a.shape, mybir.dt.from_np(a.dtype), kind="ExternalInput").ap())
    out = nc.dram_tensor("out_x", (1250, 512), F32, kind="ExternalOutput").ap()
    gnn_ffn(nc, *args, out)
    r = run_bass_kernel_spmd(nc, [arrays], core_ids=[0])
    return r.results[0]["out_x"]
```

```python
from contextlib import ExitStack

import concourse.bass as bass
from concourse import mybir

F32 = mybir.dt.float32
F16 = mybir.dt.float16
F32R = mybir.dt.float32r
I32 = mybir.dt.int32
U32 = mybir.dt.uint32
ALU = mybir.AluOpType
ACT = mybir.ActivationFunctionType
AX = mybir.AxisListType

P = 128
BANK = 512
EPS = 1e-5
REMOVED = -3.0e38


def gnn_ffn(nc, x, src, dst, edge, Wm, bm, Wu, bu, gamma, beta, pos_w, pos_b, qkv_w, qkv_b, wo_w, wo_b, out):
    N, D = x.shape
    E = edge.shape[0]
    TP = 125
    NT = N // TP
    FC = D // P
    HEADS, HD = 8, 64
    G = 2
    BE = G * P
    NB = -(-E // BE)
    LAST = E - BE
    SEEN = (NB - 1) * BE - LAST
    R = 4
    PATH = 88
    ALL = 792
    TAB = 800
    TOPK = 16
    SCALE = float(D) ** -0.5
    VW = HD + 1
    assert NT * TP == N and D == FC * P and SEEN % G == 0
    assert PATH >= NB + NT - 1 and PATH % R == 0 and ALL >= NB * NT and (ALL - PATH) % R == 0

    x_v = x.rearrange("(t p) d -> p t d", p=TP)
    out_v = out.rearrange("(t p) d -> t p d", p=TP)
    xn_d = nc.dram_tensor("xn_rows", (N, D), F32).ap()
    xn_v = xn_d.rearrange("(t p) d -> p t d", p=TP)
    row = lambda v: v.rearrange("(a d) -> a d", a=1)
    col = lambda v: v.rearrange("(c p) -> p c", p=P)

    def tile_of(ap, t):
        if isinstance(t, int):
            return ap[:, t, :]
        return ap[:, bass.ds(t, 1), :].rearrange("p a d -> p (a d)")

    def wait(eng, sem, value):
        if not (isinstance(value, int) and value <= 0):
            eng.wait_ge(sem, value)

    with ExitStack() as whole:
        def sem(name):
            return whole.enter_context(nc.semaphore(name))

        def sb(name, shape, dt=F32, stack=whole):
            return stack.enter_context(nc.sbuf_tensor(name, shape, dt))

        ps = whole.enter_context(nc.psum_tensor("ps", [P, 8 * BANK], F32))

        def bank(b, n=BANK, parts=P):
            return ps[0:parts, b * BANK:b * BANK + n]

        x_sb = sb("x_sb", [TP, NT, D])
        wqT = sb("wqT", [P, FC, D])
        wkvT = sb("wkvT", [P, FC, 2 * D])
        woT = sb("woT", [P, FC, D])
        xaT = sb("xaT", [P, FC, N])
        wu2T = xaT[:, :, :].rearrange("p c n -> p (c n)")[:, 0:FC * D].rearrange("p (c n) -> p c n", c=FC)
        gamma_b = sb("gamma_b", [TP, D])
        beta_b = sb("beta_b", [TP, D])
        late = sb("late", [P, 2, D])
        wob_b, vb_b = late[0:TP, 0, :], late[0:TP, 1, :]
        ident = sb("ident", [P, P])
        ones = sb("ones", [P, P])
        kb = sb("kb", [P, FC])
        cw = sb("cw", [P, FC, 3])
        cw1 = sb("cw1", [P, FC])
        pb = sb("pb", [P, FC])
        bmc = sb("bmc", [P, FC])
        brhs = sb("brhs", [P, D])

        gnn = ExitStack()
        g_sb = lambda n, s, d=F32: sb(n, s, d, gnn)
        xn = g_sb("xn", [TP, NT, D])
        w1T = g_sb("w1T", [P, FC, D])
        w2T = g_sb("w2T", [P, FC, D])
        ring = g_sb("ring", [P, R, G * D])
        onehot = g_sb("onehot", [P, R, G, TP])
        iota_n = g_sb("iota_n", [P, NT, TP], F16)
        tab_b = g_sb("tab_b", [1, TAB], I32)
        tab_e = g_sb("tab_e", [1, TAB], I32)
        tab_t = g_sb("tab_t", [1, TAB], I32)
        dst_i = g_sb("dst_i", [P, NB + 1, G], I32)
        dst_f = g_sb("dst_f", [P, NB + 1, G])
        src_i = g_sb("src_i", [P, NB + 1, G], I32)
        idx = g_sb("idx", [P, R, G], I32)
        seq_a = g_sb("seq_a", [TP, E // TP], I32)
        seq_b = g_sb("seq_b", [TP, E // TP], I32)
        falls = g_sb("falls", [TP, E // TP])
        fall = g_sb("fall", [TP, 1])
        dl_i = g_sb("dl_i", [1, NB], I32)
        dl_f = g_sb("dl_f", [1, NB])
        thr = g_sb("thr", [PATH, NB])
        below = g_sb("below", [PATH, NB])
        stepped = g_sb("stepped", [PATH, 1])
        rows = g_sb("rows", [1, 6, PATH])
        flag_f = g_sb("flag_f", [1, 1])
        flag_i = g_sb("flag_i", [1, 1], I32)
        natB = g_sb("natB", [P, 4, D])
        acc = g_sb("acc", [TP, NT, D + 1])
        natA = g_sb("natA", [P, 8, D])
        mv = g_sb("mv", [TP, NT, 2])
        st6 = g_sb("st6", [TP, NT, 6])
        sd = g_sb("sd", [TP, NT])
        rs = g_sb("rs", [TP, NT])
        rcnt = g_sb("rcnt", [TP, NT])
        cnt1 = g_sb("cnt1", [TP, NT])
        has = g_sb("has", [TP, NT])
        blhs = g_sb("blhs", [P, 2, TP])
        tiny = g_sb("tiny", [TP, 2, 1])
        ln = natA[0:TP, 0:4, :]
        xs = natA[0:TP, 4:6, :]
        sc = natA[0:TP, 6:8, :]
        k_low = natA[:, 4:8, :]
        lT = natB[:, :, :].rearrange("p a n -> p (a n)")[:, 0:2 * FC * TP]\
            .rearrange("p (u c n) -> p u c n", u=2, c=FC)
        gnn.close()

        ffn = ExitStack()
        f_sb = lambda n, s, d=F32: sb(n, s, d, ffn)
        xcT = f_sb("xcT", [P, FC, N + TP])
        k_parts = f_sb("k_parts", [P, HEADS, N], F32R)
        v_sb = f_sb("v_sb", [TP, NT, HEADS * VW])
        q_parts = f_sb("q_parts", [P, 2, 2, HEADS, TP], F32R)
        wkv_flat = wkvT[0:TP, :, :].rearrange("p c n -> p (c n)")
        counted_out = wkv_flat[:, 2 * D:2 * D + N]
        o_sb = wkv_flat[:, 0:2 * D].rearrange("p (s n) -> p s n", s=2)
        rS = f_sb("rS", [TP, 4, N])
        pT = f_sb("pT", [TP, NT, TP])
        oT = late[:, :, 0:FC * TP].rearrange("p u (c n) -> p u c n", c=FC)
        res = (gamma_b, beta_b)
        top = f_sb("top", [TP, 2, 16])
        rinv = f_sb("rinv", [TP, 2, 1])
        negm = f_sb("negm", [TP, 2, 1])
        sS, eS = (xaT[0:TP, :, :].rearrange("p c n -> p (c n)")[:, 2 * i * N:2 * (i + 1) * N]
                  .rearrange("p (s n) -> p s n", s=2) for i in range(2))
        logits_fast = (sS[:, 0, :], sS[:, 1, :], rS[:, 2, :], rS[:, 3, :])
        kept = f_sb("kept", [TP, 4])
        kept_all = f_sb("kept_all", [TP, 4])
        total = f_sb("total", [TP, 1])
        tied_f = f_sb("tied_f", [TP, 1])
        ties_i = f_sb("ties_i", [1, 1], I32)
        ffn.close()

        x_in = [sem(f"x_in{i}") for i in range(2)]
        idx_in = sem("idx_in")
        small_in = sem("small_in")
        wu_in = sem("wu_in")
        wm_in = sem("wm_in")
        wq_in = sem("wq_in")
        wq2_in = sem("wq2_in")
        wo_in = sem("wo_in")
        xn_out = sem("xn_out")
        consts = sem("consts")
        padded = sem("padded")
        seqpad = sem("seqpad")
        ixd = sem("ixd")
        ixp = sem("ixp")
        tabs = sem("tabs")
        acc_clear = sem("acc_clear")
        st_d = sem("st_d")
        sd_done = sem("sd_done")
        xn_done = sem("xn_done")
        xb_done = sem("xb_done")
        wt_ps = sem("wt_ps")
        wt_sb = sem("wt_sb")
        sums = sem("sums")
        load_done = [sem(f"load_done{i}") for i in range(R)]
        gather_done = [sem(f"gather_done{i}") for i in range(R)]
        idx_done = sem("idx_done")
        hot_done = sem("hot_done")
        adds = sem("adds")
        p_gate, v_gate, a_gate = sem("p_gate"), sem("v_gate"), sem("a_gate")
        u1_in = sem("u1_in")
        u1_turned = sem("u1_turned")
        u1_lhs = sem("u1_lhs")
        u1_ps = sem("u1_ps")
        u1_done = sem("u1_done")
        counted = sem("counted")
        xs_in = [sem("xs_in0"), sem("xs_in1")]
        lT_done = sem("lT_done")
        res_done = sem("res_done")
        stat_done = sem("stat_done")
        sc_done = sem("sc_done")
        norm = sem("norm")
        upT = sem("upT")
        u_ps = sem("u_ps")
        gelu_done = sem("gelu_done")
        ve_done = sem("ve_done")
        sq_done = sem("sq_done")
        x1_done = sem("x1_done")
        x1b_done = sem("x1b_done")
        xa_done = sem("xa_done")
        xaT_ps = sem("xaT_ps")
        xaT_sb = sem("xaT_sb")
        xc_done = sem("xc_done")
        vones = sem("vones")
        k_ps = sem("k_ps")
        k_high = sem("k_high")
        k_lows = sem("k_lows")
        k_moved = [sem(f"k_moved{i}") for i in range(4)]
        qb_in = sem("qb_in")
        v_ps = sem("v_ps")
        v_done = sem("v_done")

        class Path:

            def __init__(self, name):
                self.q_ps = sem(name + "q_ps")
                self.q_high = sem(name + "q_high")
                self.q_low = sem(name + "q_low")
                self.q_moved = [sem(name + "q_moved0"), sem(name + "q_moved1")]
                self.s_ps = sem(name + "s_ps")
                self.s_sb = sem(name + "s_sb")
                self.max1 = sem(name + "max1")
                self.rep1 = sem(name + "rep1")
                self.max2 = sem(name + "max2")
                self.rep2 = sem(name + "rep2")
                self.m_done = sem(name + "m_done")
                self.e_done = sem(name + "e_done")
                self.r_done = sem(name + "r_done")
                self.p_done = sem(name + "p_done")
                self.reach = sem(name + "reach")
                self.c_done = sem(name + "c_done")
                self.pT_ps = sem(name + "pT_ps")
                self.pT_sb = sem(name + "pT_sb")
                self.o_ps = sem(name + "o_ps")
                self.inv_done = sem(name + "inv_done")
                self.o_done = sem(name + "o_done")
                self.oT_ps = sem(name + "oT_ps")
                self.oT_sb = sem(name + "oT_sb")
                self.y_ps = sem(name + "y_ps")
                self.y_done = sem(name + "y_done")
                self.y_out = [sem(name + "y_out0"), sem(name + "y_out1")]

        fast, exact = Path("f_"), Path("x_")
        kept_sum = sem("kept_sum")
        tie_steps = sem("tie_steps")
        ties_ps = sem("ties_ps")
        ties_known = sem("ties_known")

        def again_if_tied(eng, attention):
            eng.wait_ge(ties_known, 1)
            tied = eng.value_load(ties_i[0:1, 0:1], min_val=0, max_val=TP)
            with eng.If(tied > 0):
                eng.wait_ge(fast.s_sb, HEADS * NT + 1)
                eng.wait_ge(fast.q_low, 2 * (NT + 1))
                eng.wait_ge(fast.q_moved[0], 64 * (NT // 2 + 1))
                eng.wait_ge(fast.q_moved[1], 64 * (NT // 2))
                for u in range(2):
                    eng.wait_ge(fast.y_out[u], 16 * NT // 2)
                attention(exact)
            eng.end_ifs()

        def gate(eng, s):
            eng.sem_inc(s, 1)

        EPN = E // TP
        GROUPS = ((0, 6), (6, NT))
        SPANS = ((0, GROUPS[0][1] * TP - 1), (GROUPS[0][1] * TP - 1, N))
        V_FIRST = SPANS[0][1] // TP
        PIECES = ((0, BANK), (BANK, 2 * BANK), (2 * BANK, N))
        K_BANKS = (0, 1, 2, 4)
        assert PIECES[0][1] <= SPANS[0][1] and NT - V_FIRST == 5
        block = whole.enter_context(nc.Block())

        @block.sync
        def _(sp):
            for h in range(2):
                t0, t1 = h * NT // 2, (h + 1) * NT // 2
                for a, b in ((0, 120), (120, TP)):
                    sp.dma_start(x_sb[a:b, t0:t1, :], x_v[a:b, t0:t1, :]).then_inc(x_in[h], 16)
            sp.wait_ge(xn_done, NT)
            for a, b in ((0, 120), (120, TP)):
                sp.dma_start(xn_v[a:b, :, :], xn[a:b, :, :]).then_inc(xn_out, 16)
            sp.wait_ge(tabs, 1)

            def load_items(first, end):
                with sp.Fori(first, end, R) as i:
                    for r in range(R):
                        e0 = sp.value_load(tab_e[0:1, bass.ds(i + r, 1)], min_val=0, max_val=LAST)
                        sp.wait_ge(sums, i + (r + 1))
                        sp.dma_start(ring[:, r, :], edge[bass.ds(e0, BE), :].rearrange("(p g) d -> p (g d)", g=G))\
                            .then_inc(load_done[r], 16)

            load_items(0, R)
            sp.dma_start(natA[:, 0:8, :].rearrange("p a n -> p (a n)").rearrange("p (c f) -> p c f", c=FC),
                         Wu.rearrange("(c p) f -> p c f", p=P)).then_inc(wu_in, 16)
            sp.dma_start(natB[:, :, :], Wm.rearrange("(c p) f -> p c f", p=P)).then_inc(wm_in, 16)
            load_items(R, PATH)
            unsorted = sp.value_load(flag_i[0:1, 0:1], min_val=0, max_val=1)
            with sp.If(unsorted > 0):
                load_items(PATH, ALL)
            sp.end_ifs()

            sp.wait_ge(u1_done, NT)
            with sp.Fori(0, NT // 2) as pair:
                for u in range(2):
                    sp.wait_ge(res_done, 2 * pair + (u + 1))
                    sp.dma_start(xs[:, u, :], xn_v[:, bass.ds(2 * pair + u, 1), :].rearrange("p a d -> p (a d)"))\
                        .then_inc(xs_in[u], 16)

            def attention(of):
                def spread_q(t, u):
                    sp.wait_ge(of.q_low, 2 * t + 2)
                    for o in range(2):
                        for part in range(2):
                            sp.dma_start(q_parts[HD - HD * o:P - HD * o, u, part, o:HEADS:2, :].bitcast(F32),
                                         q_parts[HD * o:HD * o + HD, u, part, o:HEADS:2, :].bitcast(F32))\
                                .then_inc(of.q_moved[u], 16)

                def store(t, u):
                    sp.wait_ge(of.y_done, t + 1)
                    dst_rows = out_v[t] if isinstance(t, int) else out_v[bass.ds(t, 1)].rearrange("a p d -> (a p) d")
                    sp.dma_start(dst_rows, res[u][:, :]).then_inc(of.y_out[u], 16)

                if of is fast:
                    for piece, (a, z) in enumerate(PIECES):
                        for c in range(FC):
                            sp.wait_ge(k_lows, 2 * (FC * piece + c) + 2)
                            for o in range(2):
                                sp.dma_start(k_parts[HD - HD * o:P - HD * o, 2 * c + o, a:z].bitcast(F32),
                                             k_low[HD * o:HD * o + HD, c, 0:z - a]).then_inc(k_moved[c], 16)
                        if piece == 1:
                            spread_q(0, 0)
                else:
                    spread_q(0, 0)
                spread_q(1, 1)
                with sp.Fori(1, NT // 2) as pair:
                    for u in range(2):
                        spread_q(2 * pair + u, u)
                        store(2 * pair + (u - 2), u)
                spread_q(NT, 0)
                store(NT - 2, 0)
                store(NT - 1, 1)
                for u in range(2):
                    sp.wait_ge(of.y_out[u], 16 * NT // 2)
                sp.wait_ge(of.q_moved[0], 64 * (NT // 2 + 1))

            attention(fast)
            again_if_tied(sp, attention)

        @block.gpsimd
        def _(pl):
            pl.memset(ident[:, :], 0.0).then_inc(consts, 1)
            pl.memset(ones[:, :], 1.0).then_inc(consts, 1)
            pl.memset(seq_b[:, :], 1 << 20).then_inc(seqpad, 1)
            pl.wait_ge(consts, 1)
            pl.affine_select(out=ident[:, :], in_=ident[:, :], compare_op=ALU.not_equal, fill=1.0, base=0,
                             pattern=[[-1, P]], channel_multiplier=1).then_inc(consts, 1)
            pl.iota(thr[:, :], pattern=[[-TP, NB]], base=0, channel_multiplier=TP,
                    allow_small_or_imprecise_dtypes=True).then_inc(consts, 1)
            pl.iota(tab_b[0:1, :], pattern=[[1, TAB // NT], [0, NT]], base=0, channel_multiplier=0).then_inc(consts, 1)
            pl.iota(tab_t[0:1, :], pattern=[[0, TAB // NT], [1, NT]], base=0, channel_multiplier=0).then_inc(consts, 1)
            pl.iota(rows[0:1, 0, :], pattern=[[1, PATH]], base=0, channel_multiplier=0,
                    allow_small_or_imprecise_dtypes=True).then_inc(consts, 1)
            pl.iota(iota_n[:, :, :], pattern=[[TP, NT], [1, TP]], base=0, channel_multiplier=0,
                    allow_small_or_imprecise_dtypes=True).then_inc(consts, 1)
            pl.memset(blhs[:, :, :], 0.0).then_inc(consts, 1)
            pl.memset(brhs[:, :], 0.0).then_inc(consts, 1)
            pl.wait_ge(consts, 10)
            pl.memset(blhs[0:1, :, :], 1.0).then_inc(consts, 1)
            pl.wait_ge(idx_in, 16 * 9)
            pl.wait_ge(ixd, 2)
            pl.affine_select(out=dst_f[:, NB - 1, :], in_=dst_f[:, NB - 1, :], compare_op=ALU.is_ge, fill=-1.0,
                             base=-(SEEN // G), pattern=[[0, G]], channel_multiplier=1).then_inc(padded, 1)
            pl.memset(dst_f[:, NB, :], -1.0).then_inc(padded, 1)
            pl.tensor_copy(src_i[:, NB, :], src_i[:, NB - 1, :]).then_inc(padded, 1)
            pl.wait_ge(padded, 3)
            pl.wait_ge(tabs, 1)
            pl.wait_ge(xn_out, 32)

            def gather_items(first, end):
                with pl.Fori(first, end, R) as i:
                    for r in range(R):
                        b = pl.value_load(tab_b[0:1, bass.ds(i + r, 1)], min_val=0, max_val=NB)
                        pl.wait_ge(load_done[r], 16 * (i // R) + 16)
                        pl.tensor_copy(idx[:, r, :], tile_of(src_i, b)).then_inc(idx_done, 1)
                        pl.wait_ge(idx_done, i + (r + 1))
                        gate(pl, p_gate)
                        for g in range(G):
                            pl.indirect_dma_start(ring[:, r, g * D:(g + 1) * D], None, xn_d[:, :],
                                                  bass.IndirectOffsetOnAxis(ap=idx[:, r, g:g + 1].bitcast(U32), axis=0),
                                                  compute_op=ALU.add).then_inc(gather_done[r], 16)

            gather_items(0, PATH)
            unsorted = pl.value_load(flag_i[0:1, 0:1], min_val=0, max_val=1)
            with pl.If(unsorted > 0):
                gather_items(PATH, ALL)
            pl.end_ifs()
            pl.wait_ge(wt_sb, 4)
            for t in range(NT):
                pl.tensor_tensor(x_sb[:, t, :], x_sb[:, t, :], beta_b[:, :], ALU.add).then_inc(xb_done, 1)

            def keep_x1(first, end):
                with pl.Fori(first, end) as t:
                    pl.wait_ge(x1_done, t + 1)
                    gate(pl, p_gate)
                    pl.tensor_tensor(tile_of(x_sb, t), tile_of(acc, t)[:, 0:D], wob_b, ALU.add).then_inc(x1b_done, 1)

            keep_x1(*GROUPS[0])
            pl.wait_ge(u_ps, NT)
            pl.memset(v_sb[:, :, :], 1.0).then_inc(vones, 1)
            pl.memset(xcT[:, :, N:N + TP], 0.0).then_inc(vones, 1)
            keep_x1(*GROUPS[1])

            def attention(of):
                def weights_fast(n, s):
                    pl.wait_ge(of.e_done, n + 1)
                    pl.wait_ge(of.reach, n + 1)
                    gate(pl, p_gate)
                    pl.tensor_tensor(eS[:, s, :], eS[:, s, :], rS[:, s, :], ALU.mult).then_inc(of.p_done, 1)

                def weights(n, s, r):
                    pl.wait_ge(of.e_done, n + 1)
                    pl.wait_ge(of.r_done, n + 1)
                    gate(pl, p_gate)
                    pl.tensor_tensor(eS[:, s, :], eS[:, s, :], rS[:, r, :], ALU.subtract).then_inc(of.p_done, 1)

                if of is fast:
                    pl.memset(kept_all[:, :], 0.0).then_inc(kept_sum, 1)
                    with pl.Fori(0, NT * HEADS, 4) as n:
                        for r in range(4):
                            weights_fast(n + r, r % 2)
                        pl.wait_ge(of.c_done, n + 4)
                        pl.wait_ge(kept_sum, n // 4 + 1)
                        gate(pl, p_gate)
                        pl.tensor_tensor(kept_all[:, :], kept_all[:, :], kept[:, :], ALU.add).then_inc(kept_sum, 1)
                else:
                    with pl.Fori(0, NT * HEADS, 4) as n:
                        for r in range(4):
                            weights(n + r, r % 2, r)

            attention(fast)
            again_if_tied(pl, attention)

        @block.scalar
        def _(act):
            row_in = lambda o, i: act.dma_start(o, i).then_inc(small_in, 16)
            act.wait_ge(seqpad, 1)
            ix = lambda o, i: act.dma_start(o, i, allow_slow_non_contiguous=True).then_inc(idx_in, 16)
            ix(seq_a[:, :], dst.rearrange("(p n) -> p n", p=TP))
            ix(seq_b[0:TP - 1, :], dst[1:1 + (TP - 1) * EPN].rearrange("(p n) -> p n", n=EPN))
            ix(seq_b[TP - 1:TP, 0:EPN - 1], row(dst[1 + (TP - 1) * EPN:E]))
            ix(dl_i[0:1, 0:NB - 1], dst[0:(NB - 1) * BE].rearrange("(a b) -> b a", b=BE)[BE - 1:BE, :])
            ix(dl_i[0:1, NB - 1:NB], row(dst[E - 1:E]))
            for tab, v in ((dst_i, dst), (src_i, src)):
                ix(tab[:, 0:NB - 1, :], v[0:(NB - 1) * BE].rearrange("(b p g) -> p b g", p=P, g=G))
                ix(tab[:, NB - 1, :], v[LAST:E].rearrange("(p g) -> p g", g=G))
            slow = lambda o, i: act.dma_start(o, i, allow_slow_non_contiguous=True).then_inc(small_in, 16)
            for j, v in enumerate((gamma, beta, wo_b, qkv_b[2 * D:3 * D])):
                row_in(w2T[0:1, j, :], row(v))
            act.wait_ge(consts, 11)
            row_in(brhs[0:1, :], row(bu))
            slow(kb[:, :], col(qkv_b[D:2 * D]))
            slow(bmc[:, :], col(bm))
            slow(pb[:, :], col(pos_b))
            slow(cw[:, :, :], pos_w.rearrange("(c p) a k -> p c (a k)", p=P))
            act.wait_ge(st_d, 2 * NT + 1)
            act.activation(sd[:, :], sd[:, :], ACT.Sqrt).then_inc(sd_done, 1)

            n = 0

            def evac(dst_ap, src_ap):
                nonlocal n
                n += 1
                act.wait_ge(wt_ps, n)
                act.activation(dst_ap, src_ap, ACT.Copy).then_inc(wt_sb, 1)

            B4 = lambda n: 4 + n % 4
            for k, o in enumerate((gamma_b[:, :], beta_b[:, :], wob_b, vb_b)):
                evac(o, bank(B4(k), D, TP))
            for c in range(FC):
                evac(w1T[:, c, :], bank(B4(4 + c)))
            for c in range(FC):
                evac(wu2T[:, c, :], bank(B4(8 + c)))
            act.dma_start(natA[:, :, :], qkv_w[0:8 * P, :].rearrange("(c p) f -> p c f", p=P)).then_inc(wq_in, 16)
            for c in range(FC):
                evac(w2T[:, c, :], bank(B4(12 + c)))
            act.dma_start(natB[:, :, :], qkv_w[8 * P:12 * P, :].rearrange("(c p) f -> p c f", p=P)).then_inc(wq2_in, 16)
            act.wait_ge(small_in, 16 * 9)
            evac(brhs[32:33, :], ps[32:33, 4 * BANK:5 * BANK])
            k = 17
            for j in range(3):
                for c in range(FC):
                    evac(wqT[:, c, :] if j == 0 else wkvT[:, c, (j - 1) * D:j * D], bank(B4(k)))
                    k += 1
                if j == 1:
                    act.dma_start(natA[:, 0:4, :], wo_w.rearrange("(c p) f -> p c f", p=P)).then_inc(wo_in, 16)

            act.wait_ge(xn_out, 32)
            with act.Fori(0, NT) as t:
                act.activation(xs[:, 0, :], tile_of(xn, t), ACT.Copy).then_inc(u1_in, 1)
                act.wait_ge(u1_turned, t + 1)
                act.activation(lT[:, 0, :, :].rearrange("p a b -> p (a b)"), bank(4, FC * TP), ACT.Copy)\
                    .then_inc(u1_lhs, 1)
                act.wait_ge(u1_ps, t + 1)
                gate(act, a_gate)
                act.activation(tile_of(xn, t), bank(5, D, TP), ACT.Copy).then_inc(u1_done, 1)

            for c in range(FC):
                evac(woT[:, c, :], bank(B4(k)))
                k += 1

            def left(t, u):
                act.wait_ge(upT, t + 1)
                wait(act, u_ps, t - 1)
                act.activation(lT[:, u, :, :].rearrange("p a b -> p (a b)"), bank(4 * u, FC * TP), ACT.Copy)\
                    .then_inc(lT_done, 1)
                act.activation(blhs[32:33, u, :], ps[32:33, (4 * u + 1) * BANK:(4 * u + 1) * BANK + TP],
                               ACT.Copy).then_inc(lT_done, 1)

            def gelu(t, u):
                act.wait_ge(u_ps, t + 1)
                if not isinstance(t, int):
                    gate(act, a_gate)
                act.activation(tile_of(acc, t)[:, 0:D], bank(4 * u + 2, D, TP), ACT.Gelu).then_inc(gelu_done, 1)

            def root(k, group):
                a, z = GROUPS[group]
                act.wait_ge(ve_done, k)
                act.activation(sd[:, a:z], sd[:, a:z], ACT.Sqrt).then_inc(sq_done, 1)

            def normed(t):
                act.wait_ge(xaT_ps, t + 1)
                act.activation(xaT[:, :, t * TP:(t + 1) * TP],
                               bank(4 * (t % 2) + 3, FC * TP).rearrange("p (c n) -> p c n", c=FC), ACT.Copy)\
                    .then_inc(xaT_sb, 1)

            left(0, 0)
            left(1, 1)
            gelu(0, 0)
            left(2, 0)
            gelu(1, 1)
            with act.Fori(1, GROUPS[0][1] // 2) as pair:
                for u in range(2):
                    left(2 * pair + (u + 1), 1 - u)
                    gelu(2 * pair + u, u)
            left(7, 1)
            gelu(6, 0)
            root(1, 0)
            left(8, 0)
            gelu(7, 1)
            left(9, 1)
            root(2, 0)
            gelu(8, 0)
            gelu(9, 1)
            for t in range(*GROUPS[0]):
                normed(t)
            root(3, 1)
            act.dma_start(brhs[0:1, :], row(qkv_b[0:D])).then_inc(qb_in, 16)

            def k_out(piece):
                a, z = PIECES[piece]
                for c in range(FC):
                    act.wait_ge(k_ps, FC * piece + c + 1)
                    for o in range(2):
                        p0, p1 = HD * o, HD * o + HD
                        act.activation(k_parts[p0:p1, 2 * c + o, a:z],
                                       ps[p0:p1, K_BANKS[c] * BANK:K_BANKS[c] * BANK + z - a],
                                       ACT.Identity, bias=kb[p0:p1, c:c + 1]).then_inc(k_high, 1)

            k_out(0)
            root(4, 1)
            for t in range(*GROUPS[1]):
                normed(t)
            k_out(1)

            act.wait_ge(x1b_done, NT)

            def attention(of):
                def q_out(t, u):
                    act.wait_ge(of.q_ps, t + 1)
                    for o in range(2):
                        a, z = HD * o, HD * o + HD
                        act.activation(q_parts[a:z, u, 0, o:HEADS:2, :],
                                       ps[a:z, 7 * BANK:7 * BANK + FC * TP].rearrange("p (c n) -> p c n", c=FC),
                                       ACT.Copy, scale=SCALE).then_inc(of.q_high, 1)

                def slot(s):
                    return logits_fast[s] if of is fast else sS[:, s % 2, :]

                def copy_logits(n, s):
                    act.wait_ge(of.s_ps, n + 1)
                    if of is fast:
                        wait(act, of.reach, n - 3)
                        wait(act, of.rep1, n - 3)
                    else:
                        wait(act, of.e_done, n - 1)
                        wait(act, of.rep1, n - 1)
                    act.activation(slot(s), ps[0:TP, 0:N], ACT.Copy).then_inc(of.s_sb, 1)

                def exp_logits(n, s):
                    act.wait_ge(of.rep1, n + 1)
                    wait(act, of.e_done if of is fast else of.r_done, n - 1)
                    act.mul(negm[:, s % 2, :], top[:, s % 2, 0:1], -1.0).then_inc(of.m_done, 1)
                    act.wait_ge(of.m_done, n + 1)
                    act.wait_ge(of.s_sb, n + 1)
                    wait(act, of.pT_ps, 3 * (n - 1))
                    act.activation(eS[:, s % 2, :], slot(s), ACT.Exp, bias=negm[:, s % 2, :]).then_inc(of.e_done, 1)

                def count(n, r):
                    act.wait_ge(of.reach, n + 1)
                    if r == 0:
                        wait(act, kept_sum, n // 4 + 1)
                    if not isinstance(n, int) or n > 0:
                        act.wait_ge(of.c_done, n)
                    gate(act, a_gate)
                    act.activation(counted_out, rS[:, r % 2, :], ACT.Copy, accum_out=kept[:, r:r + 1])\
                        .then_inc(of.c_done, 1)

                def exp_rest(n, s):
                    act.wait_ge(of.rep2, n + 1)
                    act.activation(rS[:, s, :], rS[:, s, :], ACT.Exp, bias=negm[:, s % 2, :]).then_inc(of.r_done, 1)

                def weightsT(n):
                    for g, (a, b) in enumerate(((0, 4), (4, 8), (8, NT))):
                        act.wait_ge(of.pT_ps, 3 * n + g + 1)
                        wait(act, of.o_ps, n)
                        act.activation(pT[:, a:b, :].rearrange("p a b -> p (a b)"),
                                       bank(3 + g, (b - a) * TP, TP), ACT.Copy).then_inc(of.pT_sb, 1)

                def outT(t, u):
                    act.wait_ge(of.oT_ps, t + 1)
                    wait(act, of.y_ps, t - 1)
                    act.activation(oT[:, u, :, :].rearrange("p a b -> p (a b)"), bank(7, FC * TP), ACT.Copy)\
                        .then_inc(of.oT_sb, 1)

                def tile(t, u, first=False):
                    for h in range(HEADS):
                        n = HEADS * t + h
                        if of is fast and first and h == 2:
                            act.wait_ge(v_ps, NT)
                        if not (first and h < 2):
                            if of is fast:
                                count(n - 2, (h - 2) % 4)
                            else:
                                exp_rest(n - 2, (h - 2) % 4)
                        if h == 1:
                            q_out(t + 1, 1 - u)
                        if not (first and h < 3):
                            weightsT(n - 3)
                        if h == 5 and not first:
                            outT(t - 1, 1 - u)
                        if not (first and h < 1):
                            exp_logits(n - 1, (h - 1) % 4)
                        copy_logits(n + 1, (h + 1) % 4)

                q_out(0, 0)
                if of is fast:
                    k_out(2)
                copy_logits(0, 0)
                tile(0, 0, True)
                tile(1, 1)
                with act.Fori(1, NT // 2) as pair:
                    for u in range(2):
                        tile(2 * pair + u, u)
                last = HEADS * NT
                if of is fast:
                    count(last - 2, 2)
                else:
                    exp_rest(last - 2, 2)
                weightsT(last - 3)
                exp_logits(last - 1, 3)
                if of is fast:
                    count(last - 1, 3)
                else:
                    exp_rest(last - 1, 3)
                weightsT(last - 2)
                weightsT(last - 1)
                outT(NT - 1, (NT - 1) % 2)

            attention(fast)
            again_if_tied(act, attention)

        @block.vector
        def _(dv):
            dv.sem_inc(adds, 2)
            for t in range(NT):
                dv.wait_ge(x_in[t // (NT // 2)], 32)
                dv.bn_stats(st6[:, t, :], x_sb[:, t, :]).then_inc(st_d, 1)
            for t in range(NT):
                dv.wait_ge(st_d, t + 1)
                dv.bn_aggr(mv[:, t, :], st6[:, t, :]).then_inc(st_d, 1)
            dv.wait_ge(st_d, 2 * NT)
            dv.tensor_scalar(sd[:, :], mv[:, :, 1:2].rearrange("p a b -> p (a b)"), EPS, None, ALU.add)\
                .then_inc(st_d, 1)
            dv.wait_ge(sd_done, 1)
            dv.reciprocal(rs[:, :], sd[:, :]).then_inc(st_d, 1)
            dv.wait_ge(st_d, 2 * NT + 2)
            for t in range(NT):
                dv.tensor_scalar(xn[:, t, :], x_sb[:, t, :], mv[:, t, 0:1], rs[:, t:t + 1], ALU.subtract, ALU.mult)\
                    .then_inc(xn_done, 1)

            dv.wait_ge(idx_in, 16 * 9)
            dv.tensor_copy(dl_f[:, :], dl_i[:, :]).then_inc(ixd, 1)
            dv.tensor_copy(dst_f[:, 0:NB, :], dst_i[:, 0:NB, :]).then_inc(ixd, 1)
            dv.tensor_tensor(falls[:, :], seq_a[:, :], seq_b[:, :], ALU.is_gt).then_inc(ixd, 1)
            dv.wait_ge(ixd, 3)
            dv.tensor_reduce(fall[:, :], falls[:, :], AX.X, ALU.max).then_inc(ixd, 1)
            dv.wait_ge(ixp, 1)
            dv.wait_ge(consts, 7)
            dv.tensor_tensor(below[:, :], ps[0:PATH, 7 * BANK:7 * BANK + NB], thr[:, :], ALU.is_lt).then_inc(ixd, 1)
            dv.wait_ge(ixd, 5)
            dv.tensor_reduce(stepped[:, :], below[:, :], AX.X, ALU.add).then_inc(ixd, 1)
            dv.wait_ge(ixp, 2)
            dv.tensor_scalar(flag_f[:, :], ps[0:1, 6 * BANK:6 * BANK + 1], 1.0, None, ALU.min).then_inc(ixd, 1)
            dv.wait_ge(ixd, 7)
            dv.tensor_copy(flag_i[:, :], flag_f[:, :]).then_inc(ixd, 1)
            dv.wait_ge(ixp, 3)
            b_row, t_row, db, dt_, gb, gt = (rows[0:1, j, :] for j in (1, 2, 3, 4, 5, 5))
            dv.tensor_copy(b_row, ps[0:1, 5 * BANK:5 * BANK + PATH]).then_inc(ixd, 1)
            dv.wait_ge(ixd, 9)
            dv.tensor_tensor(t_row, rows[0:1, 0, :], b_row, ALU.subtract).then_inc(ixd, 1)
            dv.wait_ge(ixd, 10)
            dv.tensor_tensor(db, tab_b[0:1, 0:PATH], b_row, ALU.subtract).then_inc(ixd, 1)
            dv.tensor_tensor(dt_, tab_t[0:1, 0:PATH], t_row, ALU.subtract).then_inc(ixd, 1)
            dv.wait_ge(ixd, 12)
            dv.scalar_tensor_tensor(gb, db, flag_f[:, 0:1], b_row, ALU.mult, ALU.add).then_inc(ixd, 1)
            dv.wait_ge(ixd, 13)
            dv.tensor_copy(tab_b[0:1, 0:PATH], gb).then_inc(ixd, 1)
            dv.wait_ge(ixd, 14)
            dv.scalar_tensor_tensor(gt, dt_, flag_f[:, 0:1], t_row, ALU.mult, ALU.add).then_inc(ixd, 1)
            dv.wait_ge(ixd, 15)
            dv.tensor_scalar(tab_t[0:1, 0:PATH], gt, float(NT - 1), 0.0, ALU.min, ALU.max).then_inc(ixd, 1)
            dv.tensor_scalar(tab_e[0:1, :], tab_b[0:1, :], float(BE), float(LAST), ALU.mult, ALU.min).then_inc(ixd, 1)
            dv.wait_ge(ixd, 17)
            dv.sem_inc(tabs, 1)

            def hot(k, r, count):
                b = dv.value_load(tab_b[0:1, bass.ds(k, 1)], min_val=0, max_val=NB)
                j = dv.value_load(tab_t[0:1, bass.ds(k, 1)], min_val=0, max_val=NT - 1)
                wait(dv, sums, count)
                if not isinstance(count, int):
                    gate(dv, v_gate)
                for g in range(G):
                    ins = dv.tensor_scalar(onehot[:, r, g, :], tile_of(iota_n, j),
                                           dst_f[:, bass.ds(b, 1), g:g + 1].rearrange("p a b -> p (a b)"), None,
                                           ALU.is_equal)
                ins.then_inc(hot_done, 1)

            def add(k, r):
                j = dv.value_load(tab_t[0:1, bass.ds(k, 1)], min_val=0, max_val=NT - 1)
                dv.wait_ge(sums, k + (R + 1))
                dv.wait_ge(adds, k + 2)
                gate(dv, v_gate)
                dv.tensor_tensor(tile_of(acc, j), tile_of(acc, j), ps[0:TP, 2 * (r % 2) * BANK:2 * (r % 2) * BANK + D + 1],
                                 ALU.add).then_inc(adds, 1)

            def sum_items(first, end):
                with dv.Fori(first, end, R) as i:
                    for r in range(R):
                        hot(i + (r + 2), (r + 2) % R, i + (r + 3))
                        add(i + r, r)

            dv.wait_ge(padded, 3)
            dv.wait_ge(consts, 8)
            dv.wait_ge(tabs, 1)
            hot(0, 0, 0)
            hot(1, 1, 0)
            dv.memset(acc[:, :, :], 0.0).then_inc(acc_clear, 1)
            dv.wait_ge(acc_clear, 1)
            sum_items(0, PATH)
            dv.wait_ge(adds, PATH + 2)
            unsorted = dv.value_load(flag_i[0:1, 0:1], min_val=0, max_val=1)
            with dv.If(unsorted > 0):
                sum_items(PATH, ALL)
                dv.wait_ge(adds, ALL + 2)
            dv.end_ifs()

            counts = acc[:, :, D:D + 1].rearrange("p a b -> p (a b)")
            dv.tensor_scalar(cnt1[:, :], counts, 1.0, None, ALU.max).then_inc(counted, 1)
            dv.tensor_scalar(has[:, :], counts, 1.0, None, ALU.min).then_inc(counted, 1)
            dv.wait_ge(counted, 1)
            dv.reciprocal(rcnt[:, :], cnt1[:, :]).then_inc(counted, 1)
            dv.wait_ge(counted, 3)
            dv.sem_inc(res_done, 2)

            def one(ap, t):
                return ap[:, t:t + 1] if isinstance(t, int) else ap[:, bass.ds(t, 1)]

            def mean(t, u):
                wait(dv, upT, t - 1)
                if not isinstance(t, int):
                    gate(dv, v_gate)
                dv.tensor_copy(tiny[:, u, :], one(has, t)).then_inc(sc_done, 1)
                dv.tensor_scalar(sc[:, u, :], tile_of(acc, t)[:, 0:D], one(rcnt, t), None, ALU.mult)\
                    .then_inc(sc_done, 1)

            def residual(t, u):
                dv.wait_ge(gelu_done, t + 1)
                dv.wait_ge(xs_in[u], 16 * (t // 2 + 1) if isinstance(t, int) else 8 * (t - u) + 16)
                gate(dv, v_gate)
                dv.tensor_tensor(tile_of(acc, t)[:, 0:D], tile_of(acc, t)[:, 0:D], xs[:, u, :], ALU.add)\
                    .then_inc(res_done, 1)
                dv.wait_ge(res_done, t + 3)
                gate(dv, v_gate)
                dv.bn_stats(tile_of(st6, t), tile_of(acc, t)[:, 0:D]).then_inc(stat_done, 1)

            steps = 0

            def own(ins):
                nonlocal steps
                ins.then_inc(norm, 1)
                steps += 1
                return steps

            def spread(group):
                a, z = GROUPS[group]
                for t in range(a, z):
                    done = own(dv.bn_aggr(mv[:, t, :], st6[:, t, :]))
                dv.wait_ge(norm, done)
                dv.tensor_scalar(sd[:, a:z], mv[:, a:z, 1:2].rearrange("p a b -> p (a b)"), EPS, None, ALU.add)\
                    .then_inc(ve_done, 1)

            def scales(k, group):
                a, z = GROUPS[group]
                dv.wait_ge(sq_done, k)
                dv.wait_ge(norm, own(dv.reciprocal(rs[:, a:z], sd[:, a:z])))

            def x1(ts):
                a_tile = lambda t: acc[:, t, 0:D]
                for t in ts:
                    done = own(dv.scalar_tensor_tensor(a_tile(t), a_tile(t), mv[:, t, 0:1], gamma_b[:, :],
                                                       ALU.subtract, ALU.mult))
                dv.wait_ge(norm, done)
                for t in ts:
                    dv.scalar_tensor_tensor(a_tile(t), a_tile(t), rs[:, t:t + 1], x_sb[:, t, :], ALU.mult, ALU.add)\
                        .then_inc(x1_done, 1)
                dv.wait_ge(x1_done, ts[-1] + 1)
                for t in ts:
                    done = own(dv.bn_stats(st6[:, t, :], a_tile(t)))
                dv.wait_ge(norm, done)

            def norm_x1(ts):
                for t in ts:
                    wait(dv, xaT_ps, t - 3)
                    dv.tensor_scalar(ln[:, t % 4, :], acc[:, t, 0:D], mv[:, t, 0:1], rs[:, t:t + 1], ALU.subtract,
                                     ALU.mult).then_inc(xa_done, 1)

            def convolve(span):
                a, z = SPANS[span]
                lo, hi = max(a, 1), min(z, N - 1)
                dv.wait_ge(xaT_sb, GROUPS[span][1])
                for cs in ((0, 1), (2, 3)):
                    for c in cs:
                        done = own(dv.tensor_scalar(xcT[:, c, a:z], xaT[:, c, a:z], cw1[:, c:c + 1], pb[:, c:c + 1],
                                                    ALU.mult, ALU.add))
                    dv.wait_ge(norm, done)
                    for c in cs:
                        done = own(dv.scalar_tensor_tensor(xcT[:, c, lo:z], xaT[:, c, lo - 1:z - 1], cw[:, c, 0:1],
                                                           xcT[:, c, lo:z], ALU.mult, ALU.add))
                    dv.wait_ge(norm, done)
                    for c in cs:
                        dv.scalar_tensor_tensor(xcT[:, c, a:hi], xaT[:, c, a + 1:hi + 1], cw[:, c, 2:3],
                                                xcT[:, c, a:hi], ALU.mult, ALU.add).then_inc(xc_done, 1)

            def k_rest(piece):
                a, z = PIECES[piece]
                for c in range(FC):
                    if piece:
                        dv.wait_ge(k_moved[c], 32 * piece)
                    dv.wait_ge(k_high, 2 * (FC * piece + c) + 2)
                    for o in range(2):
                        p0, p1 = HD * o, HD * o + HD
                        dv.scalar_tensor_tensor(k_low[p0:p1, c, 0:z - a].bitcast(F32R),
                                                ps[p0:p1, K_BANKS[c] * BANK:K_BANKS[c] * BANK + z - a],
                                                kb[p0:p1, c:c + 1], k_parts[p0:p1, 2 * c + o, a:z].bitcast(F32),
                                                ALU.add, ALU.subtract).then_inc(k_lows, 1)

            def value(t):
                dv.wait_ge(v_ps, t + 1)
                dv.tensor_tensor(v_sb[:, t, :].rearrange("p (h w) -> p h w", w=VW)[:, :, 0:HD],
                                 bank(5 + t % 2, D, TP).rearrange("p (h w) -> p h w", w=HD),
                                 vb_b.rearrange("p (h w) -> p h w", w=HD), ALU.add).then_inc(v_done, 1)

            mean(0, 0)
            mean(1, 1)
            dv.wait_ge(small_in, 16 * 9)
            dv.wait_ge(norm, own(dv.tensor_scalar(cw1[:, :], cw[:, :, 1:2].rearrange("p a b -> p (a b)"), 1.0, None, ALU.add)))
            with dv.Fori(0, GROUPS[0][1] // 2) as pair:
                for u in range(2):
                    mean(2 * pair + (u + 2), u)
                    residual(2 * pair + u, u)
            dv.wait_ge(stat_done, 6)
            spread(0)
            mean(8, 0)
            residual(6, 0)
            mean(9, 1)
            dv.wait_ge(xb_done, NT)
            scales(1, 0)
            x1((0, 1, 2))
            x1((3, 4, 5))
            spread(0)
            residual(7, 1)
            dv.wait_ge(wt_sb, 33)
            scales(2, 0)
            norm_x1((0, 1, 2))
            residual(8, 0)
            norm_x1((3, 4, 5))
            dv.wait_ge(x1b_done, GROUPS[0][1])
            residual(9, 1)
            convolve(0)
            dv.wait_ge(stat_done, NT)
            spread(1)
            scales(3, 1)
            x1((6, 7))
            x1((8, 9))
            spread(1)
            k_rest(0)
            dv.wait_ge(vones, 2)
            value(0)
            scales(4, 1)
            norm_x1((6, 7))
            value(1)
            norm_x1((8, 9))
            value(2)
            convolve(1)
            for t in range(3, V_FIRST):
                value(t)
            k_rest(1)
            dv.wait_ge(x1b_done, NT)

            def attention(of):
                def q_rest(t, u):
                    dv.wait_ge(of.q_high, 2 * t + 2)
                    for o in range(2):
                        a, z = HD * o, HD * o + HD
                        dv.scalar_tensor_tensor(q_parts[a:z, u, 1, o:HEADS:2, :],
                                                ps[a:z, 7 * BANK:7 * BANK + FC * TP].rearrange("p (c n) -> p c n", c=FC),
                                                SCALE, q_parts[a:z, u, 0, o:HEADS:2, :].bitcast(F32), ALU.mult,
                                                ALU.subtract).then_inc(of.q_low, 1)

                def slot(s):
                    return logits_fast[s] if of is fast else sS[:, s % 2, :]

                def first_eight(n, s):
                    dv.wait_ge(of.s_sb, n + 1)
                    wait(dv, of.m_done, n - 1)
                    gate(dv, v_gate)
                    dv.max(top[:, s % 2, 0:8], slot(s)).then_inc(of.max1, 1)

                def without_eight(n, s):
                    dv.wait_ge(of.max1, n + 1)
                    if of is fast:
                        wait(dv, of.p_done, n - 1)
                        wait(dv, of.c_done, n - 1)
                    else:
                        wait(dv, of.p_done, n - 3)
                    gate(dv, v_gate)
                    dv.match_replace(rS[:, s % 2 if of is fast else s, :], top[:, s % 2, 0:8], slot(s), REMOVED)\
                        .then_inc(of.rep1, 1)

                def next_eight(n, s):
                    dv.wait_ge(of.rep1, n + 1)
                    if of is fast:
                        wait(dv, of.reach, n - 1)
                    gate(dv, v_gate)
                    dv.max(top[:, s % 2, 8:16], rS[:, s % 2 if of is fast else s, :]).then_inc(of.max2, 1)

                def reach_sixteenth(n, s):
                    dv.wait_ge(of.max2, n + 1)
                    gate(dv, v_gate)
                    dv.tensor_scalar(rS[:, s % 2, :], slot(s), top[:, s % 2, 15:16], None, ALU.is_ge)\
                        .then_inc(of.reach, 1)

                def without_sixteen(n, s, r):
                    dv.wait_ge(of.max2, n + 1)
                    gate(dv, v_gate)
                    dv.match_replace(rS[:, r, :], top[:, s, 8:16], rS[:, r, :], REMOVED).then_inc(of.rep2, 1)

                def invert(n, h):
                    dv.wait_ge(of.o_ps, n + 1)
                    dv.reciprocal(rinv[:, h % 2, :], ps[0:TP, 6 * BANK + HD:6 * BANK + VW]).then_inc(of.inv_done, 1)

                def output(n, h, u):
                    dv.wait_ge(of.inv_done, n + 1)
                    dv.tensor_scalar(o_sb[:, u, h * HD:(h + 1) * HD], ps[0:TP, 6 * BANK:6 * BANK + HD],
                                     rinv[:, h % 2, :], None, ALU.mult).then_inc(of.o_done, 1)

                def result(t, u):
                    dv.wait_ge(of.y_ps, t + 1)
                    wait(dv, of.y_out[u], 16 * ((t - u) // 2) if isinstance(t, int) else 8 * (t - u))
                    gate(dv, v_gate)
                    dv.tensor_tensor(res[u][:, :], bank(7, D, TP), tile_of(x_sb, t), ALU.add).then_inc(of.y_done, 1)

                def tile(t, u, first=False):
                    for h in range(HEADS):
                        n = HEADS * t + h
                        old = not (first and h < 4)
                        if old:
                            invert(n - 4, h)
                        if of is fast and first and h == 3:
                            value(NT - 1)
                        first_eight(n, h % 4)
                        if of is fast and first and h < 3:
                            value(V_FIRST + 1 + h)
                        if h == 4:
                            wait(dv, of.oT_ps, t - 1)
                        if old:
                            output(n - 4, (h - 4) % HEADS, u if h >= 4 else 1 - u)
                        if not (first and h < 1):
                            next_eight(n - 1, (h - 1) % 4)
                        without_eight(n, h % 4)
                        if not (first and h < 1):
                            if of is fast:
                                reach_sixteenth(n - 1, (h - 1) % 4)
                            else:
                                without_sixteen(n - 1, 1 - h % 2, (h - 1) % 4)
                        if h == 1:
                            q_rest(t + 1, 1 - u)
                        if h == 7 and not first:
                            result(t - 1, 1 - u)

                q_rest(0, 0)
                if of is fast:
                    k_rest(2)
                    value(V_FIRST)
                tile(0, 0, True)
                tile(1, 1)
                with dv.Fori(1, NT // 2) as pair:
                    for u in range(2):
                        tile(2 * pair + u, u)
                last = HEADS * NT
                next_eight(last - 1, 3)
                if of is fast:
                    reach_sixteenth(last - 1, 3)
                else:
                    without_sixteen(last - 1, 1, 3)
                for k in (4, 3, 2, 1):
                    invert(last - k, HEADS - k)
                    output(last - k, HEADS - k, (NT - 1) % 2)
                    if of is fast and k == 2:
                        dv.wait_ge(kept_sum, HEADS * NT // 4 + 1)
                        dv.tensor_reduce(total[:, :], kept_all[:, :], AX.X, ALU.add).then_inc(tie_steps, 1)
                        dv.wait_ge(tie_steps, 1)
                        dv.tensor_scalar(tied_f[:, :], total[:, :], float(TOPK * HEADS * NT), None, ALU.is_gt).then_inc(tie_steps, 1)
                        dv.wait_ge(ties_ps, 1)
                        dv.tensor_copy(ties_i[:, :], ps[0:1, 0:1]).then_inc(ties_known, 1)
                result(NT - 1, (NT - 1) % 2)

            attention(fast)
            again_if_tied(dv, attention)

        @block.tensor
        def _(pe):
            pe.sem_inc(sums, R)
            pe.wait_ge(consts, 3)
            pe.wait_ge(ixd, 1)
            pe.matmul(ps[0:PATH, 7 * BANK:7 * BANK + NB], ones[0:1, 0:PATH], dl_f[0:1, :], start=True, stop=True)\
                .then_inc(ixp, 1)
            pe.wait_ge(ixd, 4)
            pe.matmul(ps[0:1, 6 * BANK:6 * BANK + 1], fall[:, 0:1], ones[0:TP, 0:1], start=True, stop=True)\
                .then_inc(ixp, 1)
            pe.wait_ge(ixd, 6)
            pe.matmul(ps[0:1, 5 * BANK:5 * BANK + PATH], stepped[:, 0:1], ident[0:PATH, 0:PATH],
                      start=True, stop=True).then_inc(ixp, 1)
            pe.wait_ge(ixd, 9)

            def sum_four(q, product=None):
                for r in range(R):
                    b = 2 * (r % 2)
                    pe.wait_ge(hot_done, R * q + (r + 1))
                    pe.wait_ge(adds, R * q + (r + 1))
                    pe.wait_ge(gather_done[r], 16 * G * q + 16 * G)
                    for g in range(G):
                        pe.matmul(ps[0:TP, b * BANK:(b + 1) * BANK], onehot[:, r, g, :],
                                  ring[:, r, g * D:(g + 1) * D], start=(g == 0), stop=(g == G - 1))
                        ins = pe.matmul(ps[0:TP, (b + 1) * BANK:(b + 1) * BANK + 1], onehot[:, r, g, :],
                                        ones[:, 0:1], start=(g == 0), stop=(g == G - 1))
                    ins.then_inc(sums, 1)
                    if product is not None and r == 0:
                        pe.wait_ge(u1_in, product)
                        for c in range(FC):
                            ins = pe.transpose(ps[:, 4 * BANK + c * TP:4 * BANK + (c + 1) * TP],
                                               xs[:, 0, c * P:(c + 1) * P], ident[0:TP, 0:TP])
                        ins.then_inc(u1_turned, 1)
                    if product is not None and r == 2:
                        pe.wait_ge(u1_lhs, product)
                        for c in range(FC):
                            ins = pe.matmul(bank(5, D, TP), lT[:, 0, c, :], w1T[:, c, :], start=(c == 0),
                                            stop=(c == FC - 1))
                        ins.then_inc(u1_ps, 1)

            def sum_items(first, end):
                with pe.Fori(first // R, end // R) as q:
                    sum_four(q)

            n = 0

            def fresh():
                nonlocal n
                if n >= 4:
                    pe.wait_ge(wt_sb, n - 3)
                n += 1
                return 4 + (n - 1) % 4

            pe.wait_ge(small_in, 16 * 9)
            for j in range(4):
                pe.matmul(bank(fresh(), D, TP), ones[0:1, 0:TP], w2T[0:1, j, :], start=True, stop=True)\
                    .then_inc(wt_ps, 1)
            sum_four(0)
            pe.wait_ge(wu_in, 16)
            wu_nat = natA[:, :, :].rearrange("p a n -> p (a n)").rearrange("p (c f) -> p c f", c=FC)
            for f in range(2 * FC):
                b = fresh()
                for o in range(FC):
                    ins = pe.transpose(ps[:, b * BANK + o * P:b * BANK + (o + 1) * P], wu_nat[:, o, f * P:(f + 1) * P],
                                       ident[:, :])
                ins.then_inc(wt_ps, 1)
            pe.wait_ge(wm_in, 16)
            for i in range(FC):
                sum_four(1 + i)
                b = fresh()
                pe.wait_ge(wt_sb, 12)
                for m in range(FC):
                    ins = pe.matmul(bank(b), natB[:, m, i * P:(i + 1) * P], wu2T[:, m, :], start=(m == 0),
                                    stop=(m == FC - 1))
                ins.then_inc(wt_ps, 1)
            sum_four(5)
            b = fresh()
            for m in range(FC):
                ins = pe.matmul(ps[32:33, b * BANK:(b + 1) * BANK], bmc[:, m:m + 1], wu2T[:, m, :], start=(m == 0),
                                stop=(m == FC - 1))
            ins.then_inc(wt_ps, 1)

            def turn(nat, first):
                for f in range(FC):
                    b = fresh()
                    for o in range(FC):
                        ins = pe.transpose(ps[:, b * BANK + o * P:b * BANK + (o + 1) * P],
                                           nat[:, first + o, f * P:(f + 1) * P], ident[:, :])
                    ins.then_inc(wt_ps, 1)

            sum_four(6)
            pe.wait_ge(wq_in, 16)
            turn(natA, 0)
            sum_four(7)
            turn(natA, 4)
            sum_four(8)
            pe.wait_ge(wq2_in, 16)
            turn(natB, 0)

            with pe.Fori(0, NT) as t:
                sum_four(t + 9, t + 1)
            sum_items((9 + NT) * R, PATH)
            unsorted = pe.value_load(flag_i[0:1, 0:1], min_val=0, max_val=1)
            with pe.If(unsorted > 0):
                sum_items(PATH, ALL)
            pe.end_ifs()
            pe.wait_ge(u1_done, NT)
            pe.wait_ge(wo_in, 16)
            turn(natA, 0)
            pe.wait_ge(wt_sb, n)

            def turn_mean(t, u):
                pe.wait_ge(sc_done, 2 * t + 2)
                wait(pe, lT_done, 2 * (t - 1))
                pe.matmul(ps[32:33, (4 * u + 1) * BANK:(4 * u + 1) * BANK + TP], tiny[:, u, :],
                          ident[0:TP, 0:TP], start=True, stop=True)
                for c in range(FC):
                    ins = pe.transpose(ps[:, 4 * u * BANK + c * TP:4 * u * BANK + (c + 1) * TP],
                                       sc[:, u, c * P:(c + 1) * P], ident[0:TP, 0:TP])
                ins.then_inc(upT, 1)

            def update(t, u):
                wait(pe, gelu_done, t - 1)
                psu = bank(4 * u + 2, D, TP)
                pe.matmul(psu, ident[0:TP, 0:TP], tile_of(xn, t), start=True, stop=False)
                pe.wait_ge(lT_done, 2 * t + 2)
                for c in range(FC):
                    pe.matmul(psu, lT[:, u, c, :], w2T[:, c, :], start=False, stop=False)
                pe.matmul(psu, blhs[:, u, :], brhs[:, :], start=False, stop=True).then_inc(u_ps, 1)

            def turn_norm(t):
                pe.wait_ge(xa_done, t + 1)
                wait(pe, xaT_sb, t - 1)
                for c in range(FC):
                    b = 4 * (t % 2) + 3
                    ins = pe.transpose(ps[:, b * BANK + c * TP:b * BANK + (c + 1) * TP],
                                       ln[:, t % 4, c * P:(c + 1) * P], ident[0:TP, 0:TP])
                ins.then_inc(xaT_ps, 1)

            turn_mean(0, 0)
            turn_mean(1, 1)
            update(0, 0)
            turn_mean(2, 0)
            update(1, 1)
            with pe.Fori(1, GROUPS[0][1] // 2) as pair:
                for u in range(2):
                    turn_mean(2 * pair + (u + 1), 1 - u)
                    update(2 * pair + u, u)
            for t in (6, 7, 8):
                turn_mean(t + 1, 1 - t % 2)
                update(t, t % 2)
            update(9, 1)
            for t in range(*GROUPS[0]):
                turn_norm(t)

            def keys(piece):
                a, z = PIECES[piece]
                for f in range(FC):
                    pe.wait_ge(xc_done, (FC if piece else 0) + f + 1)
                    for c in range(FC):
                        if piece and f == 0:
                            pe.wait_ge(k_lows, 2 * (FC * (piece - 1) + c) + 2)
                        ins = pe.matmul(ps[:, K_BANKS[c] * BANK:K_BANKS[c] * BANK + z - a],
                                        wkvT[:, f, c * P:(c + 1) * P], xcT[:, f, a:z], start=(f == 0),
                                        stop=(f == FC - 1))
                        if f == FC - 1:
                            ins.then_inc(k_ps, 1)

            def value(t):
                if t >= 2:
                    pe.wait_ge(v_done, t - 1)
                for f in range(FC):
                    ins = pe.matmul(bank(5 + t % 2, D, TP), xcT[:, f, t * TP:(t + 1) * TP], wkvT[:, f, D:2 * D],
                                    start=(f == 0), stop=(f == FC - 1))
                ins.then_inc(v_ps, 1)

            keys(0)
            for t in range(3):
                value(t)
            for t in range(*GROUPS[1]):
                turn_norm(t)
            for t in range(3, V_FIRST):
                value(t)
            keys(1)

            def attention(of):
                def queries(t):
                    wait(pe, of.y_done, t - 2)
                    for c in range(FC):
                        for f in range(FC):
                            rhs = xcT[:, f, t * TP:(t + 1) * TP] if isinstance(t, int) else xcT[:, f, bass.ds(t * TP, TP)]
                            pe.matmul(ps[:, 7 * BANK + c * TP:7 * BANK + (c + 1) * TP],
                                      wqT[:, f, c * P:(c + 1) * P], rhs, start=(f == 0), stop=False)
                        ins = pe.matmul(ps[:, 7 * BANK + c * TP:7 * BANK + (c + 1) * TP], brhs[0:1, c * P:(c + 1) * P],
                                        ones[0:1, 0:TP], start=False, stop=True)
                    ins.then_inc(of.q_ps, 1)

                def logits(n, t, h, u):
                    if h == 0:
                        pe.wait_ge(of.q_moved[u], 64 * (t // 2 + 1) if isinstance(t, int) else 32 * (t - u) + 64)
                    wait(pe, of.s_sb, n)
                    for part in range(2):
                        for a, z in PIECES:
                            ins = pe.matmul(ps[0:TP, a:z], q_parts[:, u, part, h, :], k_parts[:, h, a:z],
                                            start=(part == 0), stop=(part == 1))
                    ins.then_inc(of.s_ps, 1)

                def turn_weights(n, s):
                    pe.wait_ge(of.p_done, n + 1)
                    for g, (a, b) in enumerate(((0, 4), (4, 8), (8, NT))):
                        wait(pe, of.pT_sb, 3 * (n - 1) + g + 1)
                        for k in range(a, b):
                            ins = pe.transpose(ps[0:TP, (3 + g) * BANK + (k - a) * TP:(3 + g) * BANK + (k - a + 1) * TP],
                                               eS[:, s, k * TP:(k + 1) * TP], ident[0:TP, 0:TP])
                        ins.then_inc(of.pT_ps, 1)

                def values(n, h):
                    wait(pe, of.o_done, n)
                    for g, (a, b) in enumerate(((0, 4), (4, 8), (8, NT))):
                        pe.wait_ge(of.pT_sb, 3 * n + g + 1)
                        for k in range(a, b):
                            ins = pe.matmul(ps[0:TP, 6 * BANK:6 * BANK + VW], pT[:, k, :],
                                            v_sb[:, k, h * VW:(h + 1) * VW], start=(k == 0), stop=(k == NT - 1))
                    ins.then_inc(of.o_ps, 1)

                def outT(t, u):
                    pe.wait_ge(of.o_done, HEADS * (t + 1))
                    pe.wait_ge(of.q_low, 2 * (t + 2) + 2 if not isinstance(t, int) or t < NT - 1 else 2 * (NT + 1))
                    for c in range(FC):
                        ins = pe.transpose(ps[:, 7 * BANK + c * TP:7 * BANK + (c + 1) * TP], o_sb[:, u, c * P:(c + 1) * P],
                                           ident[0:TP, 0:TP])
                    ins.then_inc(of.oT_ps, 1)

                def project(t, u):
                    pe.wait_ge(of.oT_sb, t + 1)
                    for c in range(FC):
                        ins = pe.matmul(bank(7, D, TP), oT[:, u, c, :], woT[:, c, :], start=(c == 0), stop=(c == FC - 1))
                    ins.then_inc(of.y_ps, 1)

                def tile(t, u, first=False):
                    for h in range(HEADS):
                        n = HEADS * t + h
                        if first and h == 3:
                            pe.wait_ge(v_done, NT)
                        if not (first and h < 3):
                            turn_weights(n - 3, 1 - h % 2)
                        if h < HEADS - 1:
                            logits(n + 1, t, h + 1, u)
                        else:
                            logits(n + 1, t + 1, 0, 1 - u)
                        if of is fast and first and h < 3:
                            value(V_FIRST + 2 + h)
                        if not (first and h < 3):
                            values(n - 3, (h - 3) % HEADS)
                        if h == 0:
                            queries(t + 1)
                        if h == 4 and not first:
                            outT(t - 1, 1 - u)
                        if h == 5 and not first:
                            project(t - 1, 1 - u)

                pe.wait_ge(qb_in, 16)
                pe.wait_ge(vones, 2)
                queries(0)
                if of is fast:
                    keys(2)
                    value(V_FIRST)
                    value(V_FIRST + 1)
                    for moved in k_moved:
                        pe.wait_ge(moved, 32 * len(PIECES))
                logits(0, 0, 0, 0)
                tile(0, 0, True)
                tile(1, 1)
                with pe.Fori(1, NT // 2) as pair:
                    for u in range(2):
                        tile(2 * pair + u, u)
                for k in (3, 2, 1):
                    turn_weights(HEADS * NT - k, k % 2)
                    if of is fast and k == 1:
                        pe.wait_ge(of.s_sb, HEADS * NT + 1)
                        pe.wait_ge(tie_steps, 2)
                        pe.matmul(ps[0:1, 0:1], tied_f[:, :], ones[0:TP, 0:1], start=True, stop=True).then_inc(ties_ps, 1)
                    values(HEADS * NT - k, HEADS - k)
                outT(NT - 1, (NT - 1) % 2)
                project(NT - 1, (NT - 1) % 2)

            attention(fast)
            again_if_tied(pe, attention)



_INS = ["x", "src", "dst", "edge_attr_512", "L0_gnn_Wm", "L0_gnn_bm", "L0_gnn_Wu", "L0_gnn_bu", "L0_gnn_gamma",
        "L0_gnn_beta", "L0_ffn_pos_w", "L0_ffn_pos_b", "L0_ffn_qkv_w", "L0_ffn_qkv_b", "L0_ffn_wo_w", "L0_ffn_wo_b"]


def kernel(**inputs):
    import numpy as np
    from concourse import bacc
    from concourse.bass_utils import run_bass_kernel_spmd

    nc = bacc.Bacc("TRN2", target_bir_lowering=False, num_devices=1)
    arrays, args = {}, []
    for name in _INS:
        a = np.ascontiguousarray(inputs[name])
        arrays[f"in_{name}"] = a
        args.append(nc.dram_tensor(f"in_{name}", a.shape, mybir.dt.from_np(a.dtype), kind="ExternalInput").ap())
    out = nc.dram_tensor("out_x", (1250, 512), F32, kind="ExternalOutput").ap()
    gnn_ffn(nc, *args, out)
    r = run_bass_kernel_spmd(nc, [arrays], core_ids=[0])
    return r.results[0]["out_x"]
```
